# Optimizing a Trainium2 kernel written in Bass

```python
import numpy as np
import jax
import jax.numpy as jnp

def _softmax(x, axis=-1):
    return jax.nn.softmax(x, axis=axis)

def _gelu(x):
    return jax.nn.gelu(x, approximate=True)

def _silu(x):
    return jax.nn.silu(x)

def _sigmoid(x):
    return jax.nn.sigmoid(x)

def _layernorm(x, axis=-1, eps=1e-05):
    m = jnp.mean(x, axis=axis, keepdims=True)
    v = jnp.var(x, axis=axis, keepdims=True)
    return (x - m) / jnp.sqrt(v + eps)

def _scatter_add(tgt, idx, src, axis=0):
    return tgt.at[idx].add(src)

def _segment_sum(src, seg, n):
    return jax.ops.segment_sum(src, seg, n)
kernel_name = 'mk_xattn_ffn_d1_seqx_r2_817f7c'

def setup_inputs(seed: int=0):
    np.random.seed(seed)
    _w = jnp.asarray

    def _rec_inputs():
        import jax
        import jax.numpy as jnp
        _rk = jax.random.key(seed)
        x = 6.313e-05 + 0.9998 * jax.random.normal(jax.random.fold_in(_rk, 1), (4, 1024, 512), jnp.float32)
        _lenS = 1024 - jax.random.randint(jax.random.fold_in(_rk, 7), (4,), 0, max(1, 1024 // 4) + 1, jnp.int32)
        _lenS2 = 1024 - jax.random.randint(jax.random.fold_in(_rk, 8), (4,), 0, max(1, 1024 // 4) + 1, jnp.int32)
        _ctx_1024P = jax.random.normal(jax.random.fold_in(_rk, 11), (4, 16, 512), jnp.float32)
        _ctx_1024c = jax.random.dirichlet(jax.random.fold_in(_rk, 511), 0.3 * jnp.ones((16,), jnp.float32), (4, 1024))
        _ctx_1024t = jnp.einsum('bsk,bkd->bsd', _ctx_1024c, _ctx_1024P)
        _ctx_1024t = _ctx_1024t * jax.lax.rsqrt(jnp.mean(jnp.square(_ctx_1024t)) + 1e-12) * 0.953939
        ctx_1024 = -0.000214406 + 1.00034 * (_ctx_1024t + 0.3 * jax.random.normal(jax.random.fold_in(_rk, 611), (4, 1024, 512), jnp.float32))
        return (x, ctx_1024)
    x, ctx_1024 = _rec_inputs()

    def _L0_xattn_setup():
        import jax, jax.numpy as jnp
        import numpy as np
        from jax import lax
        BIG = jnp.float32(1e+30)

        def _pairwise_euclidean(a, b):
            aa = jnp.sum(a * a, axis=-1)[:, None]
            bb = jnp.sum(b * b, axis=-1)[None, :]
            ab = a @ b.T
            return jnp.sqrt(jnp.maximum(aa + bb - 2.0 * ab, 0.0))

        def _dtw_cost(D):
            row0 = jnp.cumsum(D[0])

            def row_step(prev_row, d_row):
                first = d_row[0] + prev_row[0]

                def col_step(left, inp):
                    d_ij, up, diag = inp
                    r = d_ij + jnp.minimum(jnp.minimum(up, left), diag)
                    return (r, r)
                _, rest = lax.scan(col_step, first, (d_row[1:], prev_row[1:], prev_row[:-1]))
                row = jnp.concatenate([first[None], rest])
                return (row, row)
            _, rows = lax.scan(row_step, row0, D[1:])
            return jnp.concatenate([row0[None], rows], axis=0)

        def _backtrack(R, T1, T2):
            L = T1 + T2 - 1

            def step(carry, _):
                i, j, done = carry
                valid = jnp.logical_not(done)
                cd = jnp.where((i > 0) & (j > 0), R[jnp.maximum(i - 1, 0), jnp.maximum(j - 1, 0)], BIG)
                cu = jnp.where(i > 0, R[jnp.maximum(i - 1, 0), j], BIG)
                cl = jnp.where(j > 0, R[i, jnp.maximum(j - 1, 0)], BIG)
                choice = jnp.argmin(jnp.stack([cd, cu, cl]))
                ni = jnp.where(choice <= 1, i - 1, i)
                nj = jnp.where((choice == 0) | (choice == 2), j - 1, j)
                at_origin = (i == 0) & (j == 0)
                ni = jnp.where(at_origin, 0, ni)
                nj = jnp.where(at_origin, 0, nj)
                return ((ni, nj, done | at_origin), (i, j, valid))
            init = (jnp.int32(T1 - 1), jnp.int32(T2 - 1), jnp.bool_(False))
            _, (i_idx, j_idx, valid) = lax.scan(step, init, None, length=L)
            return (i_idx, j_idx, valid)

        def _align_one(small, large):
            T_small, d = small.shape
            T_large = large.shape[0]
            D = _pairwise_euclidean(small, large)
            R = _dtw_cost(D)
            i_idx, j_idx, valid = _backtrack(R, T_small, T_large)
            contrib = small[i_idx] * valid[:, None].astype(small.dtype)
            expanded = jnp.zeros((T_large, d), dtype=small.dtype).at[j_idx].add(contrib)
            return expanded
        key = jax.random.key(seed)
        k1, k2 = jax.random.split(key)
        teacher = jax.random.normal(k1, (16, 200, 512), dtype=jnp.float32)
        student = jax.random.normal(k2, (16, 300, 512), dtype=jnp.float32)
        return {'teacher_features': teacher, 'student_features': student}
    _L0_xattn_all = _L0_xattn_setup()
    _L0_xattn_in = {k: v for k, v in _L0_xattn_all.items() if k in ()}
    del _L0_xattn_all

    def _L0_ffn_setup():
        import jax, jax.numpy as jnp
        import numpy as np
        DIM = 512

        def _reference_tuple_inner(x, W_r, W_k, W_v, mu_r, mu_k):
            B, T, C = x.shape
            x_prev = jnp.concatenate([jnp.zeros((B, 1, C), x.dtype), x[:, :-1, :]], axis=1)
            xr = mu_r * x + (1.0 - mu_r) * x_prev
            xk = mu_k * x + (1.0 - mu_k) * x_prev
            r = jax.nn.sigmoid(jnp.einsum('btc,dc->btd', xr, W_r))
            k = jnp.einsum('btc,dc->btd', xk, W_k)
            k_act = jnp.square(jax.nn.relu(k))
            out = r * jnp.einsum('btc,dc->btd', k_act, W_v)
            new_state = x[:, -1, :]
            return (out, new_state)
        key = jax.random.key(seed)
        ks = jax.random.split(key, 6)
        B, T, C = (8, 1024, DIM)
        x = jax.random.normal(ks[0], (B, T, C), dtype=jnp.float32)
        s = 1.0 / np.sqrt(C)
        W_r = jax.random.uniform(ks[1], (C, C), jnp.float32, -s, s)
        W_k = jax.random.uniform(ks[2], (C, C), jnp.float32, -s, s)
        W_v = jax.random.uniform(ks[3], (C, C), jnp.float32, -s, s)
        mu_r = jax.random.uniform(ks[4], (C,), jnp.float32)
        mu_k = jax.random.uniform(ks[5], (C,), jnp.float32)
        return {'x': x, 'W_r': W_r, 'W_k': W_k, 'W_v': W_v, 'mu_r': mu_r, 'mu_k': mu_k}
    _L0_ffn_all = _L0_ffn_setup()
    _L0_ffn_in = {k: v for k, v in _L0_ffn_all.items() if k in ('W_r', 'W_k', 'W_v', 'mu_r', 'mu_k')}
    del _L0_ffn_all
    return {'x': x, 'ctx_1024': ctx_1024, 'L0_ffn_W_r': _L0_ffn_in['W_r'], 'L0_ffn_W_k': _L0_ffn_in['W_k'], 'L0_ffn_W_v': _L0_ffn_in['W_v'], 'L0_ffn_mu_r': _L0_ffn_in['mu_r'], 'L0_ffn_mu_k': _L0_ffn_in['mu_k']}

def reference(x, ctx_1024, L0_ffn_W_r, L0_ffn_W_k, L0_ffn_W_v, L0_ffn_mu_r, L0_ffn_mu_k):
    import jax
    import jax.numpy as jnp

    def _L0_xattn_ref(teacher_features, student_features):
        import jax, jax.numpy as jnp
        import numpy as np
        from jax import lax
        BIG = jnp.float32(1e+30)

        def _pairwise_euclidean(a, b):
            aa = jnp.sum(a * a, axis=-1)[:, None]
            bb = jnp.sum(b * b, axis=-1)[None, :]
            ab = a @ b.T
            return jnp.sqrt(jnp.maximum(aa + bb - 2.0 * ab, 0.0))

        def _dtw_cost(D):
            row0 = jnp.cumsum(D[0])

            def row_step(prev_row, d_row):
                first = d_row[0] + prev_row[0]

                def col_step(left, inp):
                    d_ij, up, diag = inp
                    r = d_ij + jnp.minimum(jnp.minimum(up, left), diag)
                    return (r, r)
                _, rest = lax.scan(col_step, first, (d_row[1:], prev_row[1:], prev_row[:-1]))
                row = jnp.concatenate([first[None], rest])
                return (row, row)
            _, rows = lax.scan(row_step, row0, D[1:])
            return jnp.concatenate([row0[None], rows], axis=0)

        def _backtrack(R, T1, T2):
            L = T1 + T2 - 1

            def step(carry, _):
                i, j, done = carry
                valid = jnp.logical_not(done)
                cd = jnp.where((i > 0) & (j > 0), R[jnp.maximum(i - 1, 0), jnp.maximum(j - 1, 0)], BIG)
                cu = jnp.where(i > 0, R[jnp.maximum(i - 1, 0), j], BIG)
                cl = jnp.where(j > 0, R[i, jnp.maximum(j - 1, 0)], BIG)
                choice = jnp.argmin(jnp.stack([cd, cu, cl]))
                ni = jnp.where(choice <= 1, i - 1, i)
                nj = jnp.where((choice == 0) | (choice == 2), j - 1, j)
                at_origin = (i == 0) & (j == 0)
                ni = jnp.where(at_origin, 0, ni)
                nj = jnp.where(at_origin, 0, nj)
                return ((ni, nj, done | at_origin), (i, j, valid))
            init = (jnp.int32(T1 - 1), jnp.int32(T2 - 1), jnp.bool_(False))
            _, (i_idx, j_idx, valid) = lax.scan(step, init, None, length=L)
            return (i_idx, j_idx, valid)

        def _align_one(small, large):
            T_small, d = small.shape
            T_large = large.shape[0]
            D = _pairwise_euclidean(small, large)
            R = _dtw_cost(D)
            i_idx, j_idx, valid = _backtrack(R, T_small, T_large)
            contrib = small[i_idx] * valid[:, None].astype(small.dtype)
            expanded = jnp.zeros((T_large, d), dtype=small.dtype).at[j_idx].add(contrib)
            return expanded
        return jax.vmap(_align_one)(teacher_features, student_features)

    def _L0_ffn_ref(x, W_r, W_k, W_v, mu_r, mu_k):
        import jax, jax.numpy as jnp
        import numpy as np
        DIM = 512

        def _reference_tuple_inner(x, W_r, W_k, W_v, mu_r, mu_k):
            B, T, C = x.shape
            x_prev = jnp.concatenate([jnp.zeros((B, 1, C), x.dtype), x[:, :-1, :]], axis=1)
            xr = mu_r * x + (1.0 - mu_r) * x_prev
            xk = mu_k * x + (1.0 - mu_k) * x_prev
            r = jax.nn.sigmoid(jnp.einsum('btc,dc->btd', xr, W_r))
            k = jnp.einsum('btc,dc->btd', xk, W_k)
            k_act = jnp.square(jax.nn.relu(k))
            out = r * jnp.einsum('btc,dc->btd', k_act, W_v)
            new_state = x[:, -1, :]
            return (out, new_state)
        return _reference_tuple_inner(x, W_r, W_k, W_v, mu_r, mu_k)[0]
    x = x + _L0_xattn_ref(ctx_1024, _layernorm(x, axis=-1))
    x = x + _L0_ffn_ref(_layernorm(x, axis=-1), L0_ffn_W_r, L0_ffn_W_k, L0_ffn_W_v, L0_ffn_mu_r, L0_ffn_mu_k)
    return x

_drawn_inputs = setup_inputs


def setup_inputs(seed=0):
    import zlib

    import numpy as np

    out = dict(_drawn_inputs(seed))
    spreads = {}
    factors = {'L0_ffn_W_r': 4.055, 'L0_ffn_mu_r': 8.0}
    for name, (base, spread) in spreads.items():
        noise = np.random.default_rng([zlib.crc32(name.encode()), seed]).standard_normal(out[name].shape)
        drawn = base * np.exp(spread * noise) if base else spread * noise
        out[name] = jnp.asarray(drawn.astype(out[name].dtype))
    for name, factor in factors.items():
        out[name] = (out[name] * factor).astype(out[name].dtype)
    return out
```

```python
import concourse.bass as bass
from concourse import mybir
from contextlib import ExitStack

FP32 = mybir.dt.float32
BF16 = mybir.dt.bfloat16
ALU = mybir.AluOpType
ACT = mybir.ActivationFunctionType

B, N, C = 4, 1024, 512
P = 128
KC = C // P
SEG, W = P // B, N * B // P
SKEW = 3
PAD = SKEW * (SEG - 1)
TB = 80
STEPS = 2 * TB
NT = 1120
NBLK = NT // TB
PITCH = 1216
IB = 128
NIB = N // IB
JT = N // P
RR = 16
BIG = 1e30
DIAG, UP = 128.0, 129.0
MAGIC = 12582912.0
NTILE = B * N // P
GT = 4
NG = NTILE // GT
assert NT % STEPS == 0 and NT >= N + PAD and PITCH >= PAD + NT and STEPS % RR == 0 and TB % 2 == 0


def pair(buf, r, lo, hi):
    ring = buf.shape[1]
    r %= ring
    if r == ring - 1:
        return buf[:, ring - 1::-(ring - 1), lo:hi]
    return buf[:, r:r + 2, lo:hi]


def dtw_ffn_kernel(nc, x, ctx_in, w_r, w_k, w_v, mu_r, mu_k, out):
    with ExitStack() as es:
        def sb(name, shape, dt=FP32):
            return es.enter_context(nc.sbuf_tensor(name, shape, dt))

        def sem(name):
            return es.enter_context(nc.semaphore(name))

        d_scr = nc.dram_tensor("d_scratch", (B * N, PITCH), FP32, kind="Internal").ap()
        cnt_scr = nc.dram_tensor("count_scratch", (2 * P, NT), FP32, kind="Internal").ap()

        reg_a = sb("reg_a", [P, KC * B * N])
        reg_b = sb("reg_b", [P, 12480])
        reg_c = sb("reg_c", [P, (NT + 2) * (W + 1) // 2])
        ident = sb("ident", [P, P])
        identb = sb("identb", [P, P], BF16)
        eps = sb("eps", [P, 1])
        tiny = sb("tiny", [P, 1])
        magic = sb("magic", [P, 2])
        mu = sb("mu", [P, 2, KC])
        omu = sb("omu", [P, 2, KC])
        iota1 = sb("iota1", [P, N])
        bsel = sb("bsel", [P, B])
        bsrow = sb("bsrow", [B, B, P])
        sqj = sb("sqj", [P, C])
        aa = sb("aa", [P, B])
        aaT = sb("aaT", [B, IB])
        bb = sb("bb", [P, NTILE])
        stat = sb("stat", [P, GT, 6])
        mv = sb("mv", [P, 2, GT, 2])
        sd = sb("sd", [P, 2, GT])
        rstd = sb("rstd", [P, 2, GT])
        rrow = sb("rrow", [P, RR, W + 2])
        mrow = sb("mrow", [P, RR, W + 1])
        yrow = sb("yrow", [P, 2, W], BF16)
        zrow = sb("zrow", [P, 2, W], BF16)
        padm = sb("padm", [P, NT - N], BF16)
        cmid = sb("cmid", [P, TB])
        path = sb("path", [P, 2, NIB, B])
        tpre = sb("tpre", [P, 2, N], BF16)

        def part(region, at, n, pattern=None, dt=FP32, **dims):
            a = region[:, at:at + n]
            if dt != FP32:
                a = a.bitcast(dt)
            return a.rearrange(pattern, **dims) if pattern else a

        xnT = part(reg_a, 0, KC * B * N, "p (k t) -> p k t", k=KC)
        wT = part(reg_a, 0, 3 * KC * C, "p (m k c) -> p m k c", m=3, k=KC)
        pm = part(reg_a, 6144, N * NIB, "p (a i j) -> p a i j", BF16, a=2, i=NIB)
        cun = part(reg_a, 14336, 2 * N, "p (q i) -> p q i", q=2)
        xs = part(reg_b, 0, 2 * GT * C, "p (a q c) -> p a q c", a=2, q=GT)
        ctxn = part(reg_b, 0, B * C, "p (b c) -> p b c", b=B)
        ctxT = part(reg_b, 2048, KC * B * IB, "p (k t) -> p k t", k=KC)
        dstage = part(reg_b, 4096, 2 * JT * IB, "p (a g c) -> p a g c", a=2, g=JT)
        drelu = part(reg_b, 6144, JT * IB, "p (g c) -> p g c", g=JT)
        dring = part(reg_b, 7168, 2 * (W + 1) * TB, "p (a w t) -> p a w t", a=2, w=W + 1)
        tring = part(reg_b, 0, STEPS * (W + 1) // 2, "p (t w) -> p t w", BF16, t=STEPS)
        ering = part(reg_b, 2640, STEPS * (W + 2) // 2, "p (t w) -> p t w", BF16, t=STEPS)
        wnat = part(reg_b, 5360, KC * C, "p (a c) -> p a c", a=KC)
        cnt = part(reg_b, 10240, 2 * NT, "p (q t) -> p q t", q=2)
        ctxb = part(reg_b, 0, NIB * C, "p (i c) -> p i c", i=NIB)
        parts = part(reg_b, 4096, 3 * NIB * C // 2, "p (q i c) -> p q i c", BF16, q=3, i=NIB)
        choice = part(reg_c, 0, (NT + 2) * (W + 1) // 2, "p (t w) -> p t w", BF16, t=NT + 2)
        xg = part(reg_c, 0, 2 * GT * C, "p (a q c) -> p a q c", a=2, q=GT)
        xn2 = part(reg_c, 4096, GT * C, "p (q c) -> p q c", q=GT)
        xT = part(reg_c, 6144, KC * (C + 1), "p (k t) -> p k t", k=KC)
        shift = part(reg_c, 8200, 2 * C, "p (a t) -> p a t", a=2)
        xr = part(reg_c, 9224, KC * C, "p (k t) -> p k t", k=KC)
        xk = part(reg_c, 11272, KC * C, "p (k t) -> p k t", k=KC)
        kact = part(reg_c, 13320, KC * C, "p (k t) -> p k t", k=KC)
        sig = part(reg_c, 15368, 2 * C, "p (a t) -> p a t", a=2)
        rv = part(reg_c, 16392, 2 * C, "p (a t) -> p a t", a=2)
        krelu = part(reg_c, 17416, C)

        ps = [es.enter_context(nc.psum_tensor(f"ps{n}", [P, 512], FP32)) for n in range(8)]

        const_ready = sem("const_ready")
        pool_chain = sem("pool_chain")
        x_loaded = [sem("x_loaded0"), sem("x_loaded1")]
        mu_loaded = sem("mu_loaded")
        w_loaded = sem("w_loaded")
        ctx_loaded = sem("ctx_loaded")
        pad_written = sem("pad_written")
        stats_ready = sem("stats_ready")
        sd_ready = sem("sd_ready")
        xn_ready = sem("xn_ready")
        xt_in_psum = sem("xt_in_psum")
        xt_ready = sem("xt_ready")
        bb_ready = sem("bb_ready")
        dve_step = sem("dve_step")
        ctxt_in_psum = sem("ctxt_in_psum")
        ctxt_ready = sem("ctxt_ready")
        aa_ready = sem("aa_ready")
        aat_in_psum = sem("aat_in_psum")
        aat_ready = sem("aat_ready")
        d_in_psum = sem("d_in_psum")
        d_relu_done = sem("d_relu_done")
        d_staged = sem("d_staged")
        d_written = [sem("d_written0"), sem("d_written1")]
        d_loaded = [sem("d_loaded0"), sem("d_loaded1")]
        d_used = sem("d_used")
        fwd_done = sem("fwd_done")
        bwd_block = sem("bwd_block")
        ring_free = sem("ring_free")
        w_in_psum = sem("w_in_psum")
        w_ready = sem("w_ready")
        cnt_in_psum = sem("cnt_in_psum")
        cnt_taken = sem("cnt_taken")
        cnt_rounded = sem("cnt_rounded")
        cnt_written = sem("cnt_written")
        cun_loaded = sem("cun_loaded")
        path_in_psum = sem("path_in_psum")
        path_ready = sem("path_ready")
        pm_ready = sem("pm_ready")
        ctxb_loaded = sem("ctxb_loaded")
        hi_ready = sem("hi_ready")
        rest_ready = sem("rest_ready")
        mid_ready = sem("mid_ready")
        lo_ready = sem("lo_ready")
        exp_in_psum = sem("exp_in_psum")
        xmid_ready = sem("xmid_ready")
        xg_loaded = [sem("xg_loaded0"), sem("xg_loaded1")]
        stats2_ready = sem("stats2_ready")
        sd2_ready = sem("sd2_ready")
        xn2_ready = sem("xn2_ready")
        t2_in_psum = sem("t2_in_psum")
        t2_ready = sem("t2_ready")
        border_ready = sem("border_ready")
        xk_ready = sem("xk_ready")
        xr_ready = sem("xr_ready")
        k_in_psum = sem("k_in_psum")
        k_relu_done = sem("k_relu_done")
        k_ready = sem("k_ready")
        r_in_psum = sem("r_in_psum")
        sig_ready = sem("sig_ready")
        v_in_psum = sem("v_in_psum")
        rv_ready = sem("rv_ready")
        y_ready = sem("y_ready")
        y_written = [sem("y_written0"), sem("y_written1")]

        x_h = x.rearrange("b (g q p) c -> (b g) p q c", q=GT, p=P)
        out_h = out.rearrange("b (g q p) c -> (b g) p q c", q=GT, p=P)
        ctx_h = ctx_in.rearrange("b (n p) c -> n p b c", p=P)
        ctxb_h = ctx_in.rearrange("b (n p) c -> b p n c", p=P)
        d_h = d_scr.rearrange("(b g p) c -> b p g c", b=B, p=P)

        block = es.enter_context(nc.Block())

        @block.sync
        def _(sp):
            with nc.allow_non_contiguous_dma("mu, one value in each row"):
                for m, h in enumerate((mu_r, mu_k)):
                    sp.dma_start(mu[:, m, :], h.rearrange("(k p) -> p k", p=P)).then_inc(mu_loaded, 16)
            for g in range(NG):
                if g >= 2:
                    sp.wait_ge(xt_in_psum, GT * (g - 1))
                    sp.wait_ge(bb_ready, GT * (g - 1))
                sp.dma_start(xs[:, g % 2], x_h[g]).then_inc(x_loaded[g % 2], 16)

            def load_ctx(n):
                if n == 0:
                    sp.wait_ge(xt_in_psum, NTILE)
                    sp.wait_ge(bb_ready, NTILE)
                else:
                    sp.wait_ge(ctxt_in_psum, B * n)
                    sp.wait_ge(aa_ready, B * n)
                sp.dma_start(ctxn, ctx_h[n]).then_inc(ctx_loaded, 16)

            load_ctx(0)
            load_ctx(1)
            at = 1
            sp.wait_ge(pad_written, 32)
            for k in range(NBLK):
                last = min(NIB - 1, (TB * k + TB - 1) // IB)
                while at < min(NIB - 1, last + 1):
                    at += 1
                    load_ctx(at)
                for a in range(2):
                    sp.wait_ge(d_written[a], 16 * (B // 2) * (last + 1))
                if k >= 2:
                    sp.wait_ge(d_used, k - 1)
                for b in range(B):
                    src = bass.AP(d_scr.tensor, b * N * PITCH + PAD + TB * k,
                                  [[W * PITCH - SKEW, SEG], [PITCH, W], [1, TB]])
                    sp.dma_start(dring[SEG * b:SEG * b + SEG, k % 2, 0:W, :], src).then_inc(d_loaded[k % 2], 16)
            sp.wait_ge(fwd_done, 1)
            for m, h in enumerate((w_r, w_k, w_v)):
                if m:
                    sp.wait_ge(w_in_psum, KC * m)
                sp.dma_start(wnat, h.rearrange("(a p) c -> p a c", p=P)).then_inc(w_loaded, 16)
            sp.wait_ge(cnt_rounded, 2 * NBLK)
            for q in range(2):
                sp.dma_start(cnt_scr[q * P:q * P + P, :], cnt[:, q, :]).then_inc(cnt_written, 16)
            sp.wait_ge(cnt_written, 32)
            for q in range(2):
                for b in range(B):
                    src = bass.AP(cnt_scr.tensor, (q * P + SEG * b) * NT, [[NT + SKEW, SEG], [1, N]])
                    sp.dma_start(cun[SEG * b:SEG * b + SEG, q, :], src).then_inc(cun_loaded, 16)
            sp.wait_ge(cnt_in_psum, 2 * NBLK)
            sp.wait_ge(w_in_psum, 3 * KC)
            sp.dma_start(ctxb, ctxb_h[0]).then_inc(ctxb_loaded, 16)
            for g in range(2):
                sp.dma_start(xg[:, g], x_h[g]).then_inc(xg_loaded[g], 16)
            for g in range(NG):
                b = g // 2
                if g % 2 == 0 and b + 1 < B:
                    sp.wait_ge(lo_ready, NIB * (b + 1))
                    sp.dma_start(ctxb, ctxb_h[b + 1]).then_inc(ctxb_loaded, 16)
                sp.wait_ge(y_ready, GT * (g + 1))
                sp.dma_start(out_h[g], xg[:, g % 2]).then_inc(y_written[g % 2], 16)
                if g + 2 < NG:
                    sp.wait_ge(y_written[g % 2], 16 * (g // 2 + 1))
                    sp.dma_start(xg[:, g % 2], x_h[g + 2]).then_inc(xg_loaded[g % 2], 16)
            for a in range(2):
                sp.wait_ge(y_written[a], 16 * NG // 2)

        @block.gpsimd
        def _(pool):
            steps = [0]

            def after(ins):
                steps[0] += 1
                ins.then_inc(pool_chain, 1)
                pool.wait_ge(pool_chain, steps[0])

            zeros = part(reg_b, 8192, W * 128, "p (r c) -> p r c", r=W)
            after(pool.memset(zeros, 0.0))
            rows = d_scr.rearrange("(p r) c -> p r c", p=P)
            pool.dma_start(rows[:, :, 0:PAD], zeros[:, :, 0:PAD]).then_inc(pad_written, 16)
            pool.dma_start(rows[:, :, PAD + N:PITCH], zeros[:, :, 0:PITCH - PAD - N]).then_inc(pad_written, 16)
            after(pool.memset(ident[:, :], 0.0))
            after(pool.affine_select(out=ident[:, :], in_=ident[:, :], compare_op=ALU.not_equal, fill=1.0,
                                     base=0, pattern=[[-1, P]], channel_multiplier=1))
            after(pool.tensor_copy(identb[:, :], ident[:, :]))
            after(pool.memset(eps[:, :], 1e-5))
            after(pool.memset(tiny[:, :], 1e-34))
            after(pool.memset(magic[:, 0:1], MAGIC))
            after(pool.memset(magic[:, 1:2], -MAGIC))
            after(pool.memset(bsel[:, :], 0.0))
            for b in range(B):
                after(pool.memset(bsel[SEG * b:SEG * b + SEG, b:b + 1], 1.0))
            after(pool.memset(bsrow[:, :, :], 0.0))
            after(pool.affine_select(out=bsrow[:, :, :], in_=bsrow[:, :, :], compare_op=ALU.not_equal, fill=1.0,
                                     base=0, pattern=[[-1, B], [0, P]], channel_multiplier=1))
            after(pool.iota(iota1[:, :], pattern=[[1, N]], base=1, channel_multiplier=0,
                            allow_small_or_imprecise_dtypes=True))
            after(pool.memset(padm[:, :], UP))
            for b in range(B):
                q = padm[SEG * b:SEG * b + SEG, :]
                after(pool.affine_select(out=q, in_=q, compare_op=ALU.is_gt, fill=0.0, base=1,
                                         pattern=[[1, NT - N]], channel_multiplier=-SKEW))
            pool.wait_ge(pad_written, 32)
            after(pool.memset(dring[:, :, W, :], 0.0))
            for b in range(B):
                q = dring[SEG * b:SEG * b + SEG, :, W, :]
                after(pool.affine_select(out=q, in_=q, compare_op=ALU.not_equal, fill=BIG, base=1 - SEG,
                                         pattern=[[0, 2], [0, TB]], channel_multiplier=1))
            after(pool.memset(choice[:, :, W:W + 1], 0.0))
            pool.memset(choice[:, NT:NT + 2, 0:W], UP).then_inc(const_ready, 1)
            for b in range(B):
                for i in range(NIB):
                    pool.wait_ge(hi_ready, NIB * b + i + 1)
                    pool.tensor_tensor(ctxb[:, i], ctxb[:, i], parts[:, 0, i], ALU.subtract).then_inc(rest_ready, 1)
                for i in range(NIB):
                    pool.wait_ge(mid_ready, NIB * b + i + 1)
                    pool.tensor_tensor(parts[:, 2, i], ctxb[:, i], parts[:, 1, i], ALU.subtract).then_inc(lo_ready, 1)

        @block.scalar
        def _(act):
            act.wait_ge(const_ready, 1)
            for g in range(NG + 1):
                if g < NG:
                    act.wait_ge(stats_ready, g + 1)
                    if g >= 2:
                        act.wait_ge(xn_ready, GT * (g - 1))
                    act.activation(sd[:, g % 2], mv[:, g % 2, :, 1], ACT.Sqrt, bias=eps[:, 0:1]).then_inc(sd_ready, 1)
                for n in range(GT * (g - 1), GT * g) if g else ():
                    act.wait_ge(xn_ready, n + 1)
                    if n:
                        act.wait_ge(bb_ready, n)
                    act.activation(sqj[:, :], xs[:, n // GT % 2, n % GT], ACT.Square,
                                   accum_out=bb[:, n:n + 1]).then_inc(bb_ready, 1)
                    act.wait_ge(xt_in_psum, n + 1)
                    act.activation(xnT[:, :, P * n:P * n + P], ps[n % 2][:, :].rearrange("p (k t) -> p k t", k=KC),
                                   ACT.Copy).then_inc(xt_ready, 1)
            squares = 0
            act.wait_ge(bb_ready, NTILE)
            for n in range(NIB):
                act.wait_ge(ctx_loaded, 16 * (n + 1))
                if n:
                    act.wait_ge(aat_in_psum, n)
                for b in range(B):
                    if squares:
                        act.wait_ge(aa_ready, squares)
                    act.activation(sqj[:, :], ctxn[:, b], ACT.Square, accum_out=aa[:, b:b + 1]).then_inc(aa_ready, 1)
                    squares += 1
                if n:
                    act.wait_ge(d_in_psum, 2 * B * n)
                for b in range(B):
                    act.wait_ge(ctxt_in_psum, B * n + b + 1)
                    act.activation(ctxT[:, :, IB * b:IB * b + IB],
                                   ps[4 + b % 2][:, :].rearrange("p (k t) -> p k t", k=KC), ACT.Copy)\
                       .then_inc(ctxt_ready, 1)
                act.wait_ge(aat_in_psum, n + 1)
                act.activation(aaT[:, :], ps[6][0:B, 0:IB], ACT.Copy, scale=-0.5).then_inc(aat_ready, 1)
                for b in range(B):
                    o = B * n + b
                    if o:
                        act.wait_ge(d_staged, o)
                    for h in range(2):
                        act.wait_ge(d_in_psum, 2 * o + h + 1)
                        for q in range(4):
                            g = 4 * h + q
                            last = act.activation(drelu[:, g], ps[2 * (b % 2) + h][:, IB * q:IB * q + IB], ACT.Relu,
                                                  bias=bb[:, JT * b + g:JT * b + g + 1], scale=-2.0)
                        last.then_inc(d_relu_done, 1)
                    act.wait_ge(d_relu_done, 2 * (o + 1))
                    if o >= 2:
                        act.wait_ge(d_written[o % 2], 16 * (o // 2))
                    act.activation(dstage[:, o % 2], drelu, ACT.Sqrt, bias=tiny[:, 0:1]).then_inc(d_staged, 1)
                    act.wait_ge(d_staged, o + 1)
                    act.dma_start(d_h[b, :, :, PAD + IB * n:PAD + IB * n + IB], dstage[:, o % 2])\
                       .then_inc(d_written[o % 2], 16)
            for n in range(3 * KC):
                act.wait_ge(w_in_psum, n + 1)
                act.activation(wT[:, n // KC, :, P * (n % KC):P * (n % KC) + P],
                               ps[4 + n % 2][:, :].rearrange("p (k t) -> p k t", k=KC), ACT.Copy).then_inc(w_ready, 1)
            for k in range(NBLK):
                lo = NT - TB * (k + 1)
                act.wait_ge(cnt_in_psum, 2 * k + 1)
                act.activation(cnt[:, 0, lo:lo + TB], ps[2 * (k % 2)][:, 0:TB], ACT.Copy).then_inc(cnt_rounded, 1)
                act.wait_ge(cnt_in_psum, 2 * k + 2)
                if k:
                    act.wait_ge(cnt_rounded, 2 * k)
                act.activation(cmid[:, :], ps[2 * (k % 2) + 1][:, 0:TB], ACT.Identity, bias=magic[:, 0:1],
                               scale=1.0 / DIAG).then_inc(cnt_taken, 1)
                act.wait_ge(cnt_taken, k + 1)
                act.activation(cnt[:, 1, lo:lo + TB], cmid[:, :], ACT.Identity, bias=magic[:, 1:2])\
                   .then_inc(cnt_rounded, 1)

            def first_parts(b):
                act.wait_ge(ctxb_loaded, 16 * (b + 1))
                if b:
                    act.wait_ge(exp_in_psum, 2 * GT * b)
                for i in range(NIB):
                    act.activation(parts[:, 0, i], ctxb[:, i], ACT.Copy).then_inc(hi_ready, 1)

            def second_parts(b):
                for i in range(NIB):
                    act.wait_ge(rest_ready, NIB * b + i + 1)
                    act.activation(parts[:, 1, i], ctxb[:, i], ACT.Copy).then_inc(mid_ready, 1)

            def deviation(g):
                act.wait_ge(stats2_ready, g + 1)
                if g >= 2:
                    act.wait_ge(xn2_ready, GT * (g - 1))
                act.activation(sd[:, g % 2], mv[:, g % 2, :, 1], ACT.Sqrt, bias=eps[:, 0:1]).then_inc(sd2_ready, 1)

            act.wait_ge(cun_loaded, 128)
            first_parts(0)
            second_parts(0)
            deviation(0)
            for g in range(NG):
                act.wait_ge(border_ready, g + 1)
                for n in range(GT * g, GT * g + GT):
                    act.wait_ge(t2_in_psum, n + 1)
                    act.activation(xT[:, :, 1 + P * (n % GT):1 + P * (n % GT) + P],
                                   ps[2 + n % 2][:, :].rearrange("p (k t) -> p k t", k=KC), ACT.Copy)\
                       .then_inc(t2_ready, 1)
                if g + 1 < NG:
                    deviation(g + 1)
                more = g % 2 == 0 and g // 2 + 1 < B
                if more:
                    first_parts(g // 2 + 1)
                if g:
                    act.wait_ge(v_in_psum, GT * g)
                for n in range(KC * g, KC * g + KC):
                    act.wait_ge(k_in_psum, n + 1)
                    if n:
                        act.wait_ge(k_ready, n)
                    act.activation(krelu, ps[4 + n % 2][:, :], ACT.Relu).then_inc(k_relu_done, 1)
                    act.wait_ge(k_relu_done, n + 1)
                    act.activation(kact[:, n % KC], krelu, ACT.Square).then_inc(k_ready, 1)
                if more:
                    second_parts(g // 2 + 1)
                for n in range(GT * g, GT * g + GT):
                    act.wait_ge(r_in_psum, n + 1)
                    if n >= 2:
                        act.wait_ge(rv_ready, n - 1)
                    act.activation(sig[:, n % 2], ps[6][:, :], ACT.Sigmoid).then_inc(sig_ready, 1)

        @block.tensor
        def _(pe):
            pe.wait_ge(const_ready, 1)
            for n in range(NTILE):
                pe.wait_ge(xn_ready, n + 1)
                if n >= 2:
                    pe.wait_ge(xt_ready, n - 1)
                for k in range(KC):
                    last = pe.transpose(ps[n % 2][:, P * k:P * k + P], xs[:, n // GT % 2, n % GT, P * k:P * k + P],
                                        ident[:, :])
                last.then_inc(xt_in_psum, 1)
            pe.wait_ge(xt_ready, NTILE)
            for n in range(NIB):
                pe.wait_ge(ctx_loaded, 16 * (n + 1))
                for b in range(B):
                    if B * n + b >= 2:
                        pe.wait_ge(ctxt_ready, B * n + b - 1)
                    for k in range(KC):
                        last = pe.transpose(ps[4 + b % 2][:, P * k:P * k + P], ctxn[:, b, P * k:P * k + P],
                                            ident[:, :])
                    last.then_inc(ctxt_in_psum, 1)
                pe.wait_ge(aa_ready, B * (n + 1))
                if n:
                    pe.wait_ge(aat_ready, n)
                pe.transpose(ps[6][0:B, 0:IB], aa[:, :], ident[:, :]).then_inc(aat_in_psum, 1)
                pe.wait_ge(ctxt_ready, B * (n + 1))
                pe.wait_ge(aat_ready, n + 1)
                for b in range(B):
                    for h in range(2):
                        o = 2 * (B * n + b) + h
                        if o >= 4:
                            pe.wait_ge(d_relu_done, o - 3)
                        for q in range(4):
                            dst = ps[2 * (b % 2) + h][:, IB * q:IB * q + IB]
                            j = N * b + P * (4 * h + q)
                            for k in range(KC):
                                pe.matmul(dst, xnT[:, k, j:j + P], ctxT[:, k, IB * b:IB * b + IB],
                                          start=(k == 0), stop=False)
                            last = pe.matmul(dst, bsrow[:, b, :], aaT[:, :], start=False, stop=True)
                        last.then_inc(d_in_psum, 1)
            for n in range(3 * KC):
                pe.wait_ge(w_loaded, 16 * (n // KC + 1))
                if n >= 2:
                    pe.wait_ge(w_ready, n - 1)
                for k in range(KC):
                    last = pe.transpose(ps[4 + n % 2][:, P * k:P * k + P], wnat[:, n % KC, P * k:P * k + P],
                                        ident[:, :])
                last.then_inc(w_in_psum, 1)
            pe.wait_ge(d_relu_done, 2 * B * NIB)
            pe.sem_inc(ring_free, 1)
            for k in range(NBLK):
                pe.wait_ge(bwd_block, k + 1)
                if k >= 2:
                    pe.wait_ge(cnt_rounded, 2 * (k - 1))
                at = TB * (k % 2)
                for q, (ring, first) in enumerate(((tring, 0), (ering, 1))):
                    for j in range(W):
                        rows = ring[:, at + TB - 1:at - 1 if at else None:-1, first + j]
                        last = pe.matmul(ps[2 * (k % 2) + q][:, 0:TB], identb[:, :], rows,
                                         start=(j == 0), stop=(j == W - 1))
                    last.then_inc(cnt_in_psum, 1)
                pe.wait_ge(cnt_in_psum, 2 * (k + 1))
                pe.sem_inc(ring_free, 1)
            pe.wait_ge(w_ready, 3 * KC)
            pe.wait_ge(cun_loaded, 128)
            for q in range(2):
                for i in range(NIB):
                    last = pe.matmul(ps[4][:, (NIB * q + i) * B:(NIB * q + i + 1) * B],
                                     cun[:, q, P * i:P * i + P], bsel[:, :], start=True, stop=True)
            last.then_inc(path_in_psum, 1)

            def expand(g):
                b = g // 2
                pe.wait_ge(pm_ready, NIB * (b + 1))
                pe.wait_ge(lo_ready, NIB * (b + 1))
                for n in range(GT * g, GT * g + GT):
                    if n >= 2:
                        pe.wait_ge(xmid_ready, n - 1)
                    j = P * (n % JT)
                    for q in range(3):
                        for i in range(NIB):
                            last = pe.matmul(ps[n % 2][:, :], pm[:, b % 2, i, j:j + P], parts[:, q, i],
                                             start=(q == i == 0), stop=(q == 2 and i == NIB - 1))
                    last.then_inc(exp_in_psum, 1)

            pe.wait_ge(path_ready, 1)
            expand(0)
            for g in range(NG):
                for n in range(GT * g, GT * g + GT):
                    pe.wait_ge(xn2_ready, n + 1)
                    if n >= 2:
                        pe.wait_ge(t2_ready, n - 1)
                    for k in range(KC):
                        last = pe.transpose(ps[2 + n % 2][:, P * k:P * k + P], xn2[:, n % GT, P * k:P * k + P],
                                            ident[:, :])
                    last.then_inc(t2_in_psum, 1)
                if g + 1 < NG:
                    expand(g + 1)
                pe.wait_ge(xk_ready, g + 1)
                for n in range(KC * g, KC * g + KC):
                    if n >= 2:
                        pe.wait_ge(k_relu_done, n - 1)
                    m = P * (n % KC)
                    for c in range(KC):
                        last = pe.matmul(ps[4 + n % 2][:, :], wT[:, 1, c, m:m + P], xk[:, c],
                                         start=(c == 0), stop=(c == KC - 1))
                    last.then_inc(k_in_psum, 1)
                pe.wait_ge(xr_ready, g + 1)
                for n in range(GT * g, GT * g + GT):
                    t = P * (n % GT)
                    if n:
                        pe.wait_ge(sig_ready, n)
                    for c in range(KC):
                        last = pe.matmul(ps[6][:, :], xr[:, c, t:t + P], wT[:, 0, c, :],
                                         start=(c == 0), stop=(c == KC - 1))
                    last.then_inc(r_in_psum, 1)
                    pe.wait_ge(k_ready, KC * (g + 1))
                    if n:
                        pe.wait_ge(rv_ready, n)
                    for c in range(KC):
                        last = pe.matmul(ps[7][:, :], kact[:, c, t:t + P], wT[:, 2, c, :],
                                         start=(c == 0), stop=(c == KC - 1))
                    last.then_inc(v_in_psum, 1)

        @block.vector
        def _(dve):
            steps = [0]

            def after(ins):
                steps[0] += 1
                ins.then_inc(dve_step, 1)
                dve.wait_ge(dve_step, steps[0])

            def stats(src, g, ready):
                for q in range(GT):
                    last = dve.bn_stats(stat[:, q], src[:, q])
                after(last)
                for q in range(GT):
                    last = dve.bn_aggr(mv[:, g % 2, q], stat[:, q])
                steps[0] += 1
                last.then_inc(dve_step, 1)
                dve.wait_ge(dve_step, steps[0])
                dve.sem_inc(ready, 1)

            def normalise(dst, src, g, sd_sem, ready):
                dve.wait_ge(sd_sem, g + 1)
                after(dve.reciprocal(rstd[:, g % 2], sd[:, g % 2]))
                for q in range(GT):
                    dve.tensor_scalar(dst[:, q], src[:, q], mv[:, g % 2, q, 0:1], rstd[:, g % 2, q:q + 1],
                                      ALU.subtract, ALU.mult).then_inc(ready, 1)

            dve.wait_ge(const_ready, 1)
            dve.wait_ge(mu_loaded, 32)
            after(dve.tensor_scalar(omu[:, :, :], mu[:, :, :], -1.0, 1.0, ALU.mult, ALU.add))
            for g in range(NG + 1):
                if g < NG:
                    dve.wait_ge(x_loaded[g % 2], 16 * (g // 2 + 1))
                    stats(xs[:, g % 2], g, stats_ready)
                if g:
                    normalise(xs[:, (g - 1) % 2], xs[:, (g - 1) % 2], g - 1, sd_ready, xn_ready)

            after(dve.memset(rrow[:, :, :], BIG))
            after(dve.memset(mrow[:, :, :], BIG))
            for b in range(B):
                after(dve.memset(rrow[SEG * b:SEG * b + 1, RR - 1, 0:1], 0.0))
            dve.sem_clear(dve_step)
            with dve.Fori(0, NT // STEPS) as it:
                for t in range(STEPS):
                    r = t % RR
                    if t % TB == 0:
                        dve.wait_ge(d_loaded[t // TB], it * (16 * B) + 16 * B)
                    if t:
                        dve.wait_ge(dve_step, 4 * t - 1)
                        if t == TB:
                            dve.sem_inc(d_used, 1)
                    dve.tensor_tensor(mrow[:, r, 0:W], rrow[:, (r - 1) % RR, 1:W + 1], rrow[:, (r - 1) % RR, 0:W],
                                      ALU.min).then_inc(dve_step, 1)
                    if t % 2 == 0:
                        dve.stream_shuffle(pair(rrow, r - 2 + SKEW, 0, 1), pair(rrow, r - 2, W + 1, W + 2),
                                           [SEG - 1] + list(range(SEG - 1))).then_inc(dve_step, 1)
                    else:
                        dve.tensor_tensor(zrow[:, :, :], pair(mrow, r - 3, 0, W), pair(rrow, r - 3, 0, W),
                                          ALU.is_le).then_inc(dve_step, 1)
                    dve.wait_ge(dve_step, 4 * t + 1)
                    dve.tensor_tensor_scan(rrow[:, r, 1:W + 2], mrow[:, r, :], dring[:, t // TB, :, t % TB],
                                           rrow[:, r, 0:1], ALU.min, ALU.add).then_inc(dve_step, 1)
                    if t % 2 == 0:
                        dve.tensor_tensor(yrow[:, :, :], pair(rrow, r - 3, 1, W + 1), pair(rrow, r - 3, 0, W),
                                          ALU.is_lt).then_inc(dve_step, 1)
                    else:
                        dve.wait_ge(dve_step, 4 * t + 2)
                        dve.scalar_tensor_tensor(choice[:, bass.ds(it * STEPS + (t - 1), 2), 0:W], yrow[:, :, W - 1::-1], DIAG,
                                                 zrow[:, :, W - 1::-1], ALU.add, ALU.mult).then_inc(dve_step, 1)
                dve.wait_ge(dve_step, 4 * STEPS)
                dve.sem_inc(d_used, 1)
                dve.sem_clear(dve_step)
            dve.tensor_tensor(choice[:, N + 2:NT + 2, 0:W], choice[:, N + 2:NT + 2, 0:W],
                              padm[:, :].unsqueeze(2).broadcast_to([P, NT - N, W]), ALU.max).then_inc(dve_step, 1)
            dve.wait_ge(d_staged, B * NIB)
            for a in range(2):
                dve.wait_ge(d_written[a], 16 * B * NIB // 2)
            dve.memset(tring[:, :, :], 1.0).then_inc(dve_step, 1)
            dve.memset(ering[:, :, :], 0.0).then_inc(dve_step, 1)
            dve.wait_ge(dve_step, 3)
            for b in range(B):
                dve.memset(tring[SEG * b:SEG * b + 1, :, W:W + 1], 0.0).then_inc(dve_step, 1)
            dve.wait_ge(dve_step, 7)
            dve.sem_inc(fwd_done, 1)
            dve.sem_clear(dve_step)

            with dve.Fori(0, NT // STEPS) as it:
                for u in range(STEPS):
                    n = 5 * (u // 2) + 3 * (u % 2)
                    if u:
                        dve.wait_ge(dve_step, n)
                        if u == TB:
                            dve.sem_inc(bwd_block, 1)
                    if u % TB == TB - 3:
                        dve.wait_ge(ring_free, it * 2 + (u // TB + 1))
                    dve.tensor_tensor_scan(ering[:, u, 1:W + 2], choice[:, bass.ds(it * -STEPS + (NT + 1 - u), 1), :]
                                           .rearrange("p t w -> p (t w)"),
                                           tring[:, u, :], ering[:, u, 0:1], ALU.max, ALU.mult).then_inc(dve_step, 1)
                    if u % 2 == 0:
                        dve.stream_shuffle(pair(ering, u - 2 + SKEW, 0, 1), pair(ering, u - 2, W + 1, W + 2),
                                           list(range(1, SEG)) + [0]).then_inc(dve_step, 1)
                    dve.wait_ge(dve_step, n + 1)
                    dve.scalar_tensor_tensor(tring[:, (u + 1) % STEPS, 0:W], ering[:, u, 1:W + 1], DIAG,
                                             ering[:, u, 0:W], ALU.is_gt, ALU.logical_or).then_inc(dve_step, 1)
                dve.wait_ge(dve_step, 5 * STEPS // 2)
                dve.sem_inc(bwd_block, 1)
                dve.sem_clear(dve_step)
            steps[0] = 0
            dve.wait_ge(path_in_psum, 1)
            after(dve.tensor_copy(path[:, :, :, :].rearrange("p q i b -> p (q i b)"), ps[4][:, 0:2 * NIB * B]))
            dve.sem_inc(path_ready, 1)

            def build(b):
                if b >= 2:
                    dve.wait_ge(exp_in_psum, 2 * GT * (b - 1))
                for i in range(NIB):
                    if NIB * b + i >= 2:
                        dve.wait_ge(pm_ready, NIB * b + i - 1)
                    after(dve.tensor_scalar(tpre[:, i % 2], iota1[:, :], path[:, 1, i, b:b + 1], None, ALU.is_ge))
                    dve.scalar_tensor_tensor(pm[:, b % 2, i], iota1[:, :], path[:, 0, i, b:b + 1], tpre[:, i % 2],
                                             ALU.is_le, ALU.mult).then_inc(pm_ready, 1)

            def mid(g):
                dve.wait_ge(xg_loaded[g % 2], 16 * (g // 2 + 1))
                for n in range(GT * g, GT * g + GT):
                    dve.wait_ge(exp_in_psum, n + 1)
                    dve.tensor_tensor(xg[:, g % 2, n % GT], xg[:, g % 2, n % GT], ps[n % 2][:, :], ALU.add)\
                       .then_inc(xmid_ready, 1)
                dve.wait_ge(xmid_ready, GT * (g + 1))
                stats(xg[:, g % 2], g, stats2_ready)
                if g:
                    dve.wait_ge(t2_in_psum, GT * g)
                normalise(xn2, xg[:, g % 2], g, sd2_ready, xn2_ready)

            def border(g):
                if g % 2 == 0:
                    after(dve.memset(xT[:, :, 0:1], 0.0))
                else:
                    after(dve.tensor_copy(xT[:, :, 0:1], xT[:, :, C:C + 1]))
                dve.sem_inc(border_ready, 1)

            build(0)
            mid(0)
            border(0)
            for g in range(NG):
                dve.wait_ge(t2_ready, GT * (g + 1))
                for m, dst, used, ready in ((1, xk, k_in_psum, xk_ready), (0, xr, r_in_psum, xr_ready)):
                    if g:
                        dve.wait_ge(used, GT * g)
                    for c in range(KC):
                        after(dve.tensor_scalar(shift[:, c % 2], xT[:, c, 0:C], omu[:, m, c:c + 1], None, ALU.mult))
                        after(dve.scalar_tensor_tensor(dst[:, c], xT[:, c, 1:C + 1], mu[:, m, c:c + 1], shift[:, c % 2],
                                                       ALU.mult, ALU.add))
                    dve.sem_inc(ready, 1)
                if g + 1 < NG:
                    border(g + 1)
                    mid(g + 1)
                if g % 2 == 0 and g // 2 + 1 < B:
                    build(g // 2 + 1)
                for n in range(GT * g, GT * g + GT):
                    dve.wait_ge(sig_ready, n + 1)
                    dve.wait_ge(v_in_psum, n + 1)
                    dve.tensor_tensor(rv[:, n % 2], ps[7][:, :], sig[:, n % 2], ALU.mult).then_inc(rv_ready, 1)
                    dve.wait_ge(rv_ready, n + 1)
                    dve.tensor_tensor(xg[:, g % 2, n % GT], xg[:, g % 2, n % GT], rv[:, n % 2], ALU.add)\
                       .then_inc(y_ready, 1)


_INS = ["x", "ctx_1024", "L0_ffn_W_r", "L0_ffn_W_k", "L0_ffn_W_v", "L0_ffn_mu_r", "L0_ffn_mu_k"]


def kernel(**inputs):
    import numpy as _np
    import concourse.bacc as _bacc
    from concourse import mybir as _mybir
    from concourse.bass_utils import run_bass_kernel_spmd as _run

    nc = _bacc.Bacc("TRN2", target_bir_lowering=False, num_devices=1)
    arrays, args = {}, []
    for name in _INS:
        a = _np.ascontiguousarray(inputs[name])
        arrays[f"in_{name}"] = a
        args.append(nc.dram_tensor(f"in_{name}", a.shape, _mybir.dt.from_np(a.dtype), kind="ExternalInput").ap())
    out = nc.dram_tensor("out_y", (4, 1024, 512), _mybir.dt.float32, kind="ExternalOutput").ap()
    dtw_ffn_kernel(nc, *args, out)
    return _run(nc, [arrays], core_ids=[0]).results[0]["out_y"]
```

```python
import concourse.bass as bass
from concourse import mybir
from contextlib import ExitStack

FP32 = mybir.dt.float32
BF16 = mybir.dt.bfloat16
ALU = mybir.AluOpType
ACT = mybir.ActivationFunctionType

B, N, C = 4, 1024, 512
P = 128
KC = C // P
SEG, W = P // B, N * B // P
SKEW = 2
PAD = SKEW * (SEG - 1)
TB = 68
STEPS = 2 * TB
NT = 1088
NBLK = NT // TB
PITCH = 1152
IB = 128
NIB = N // IB
JT = N // P
RR = 8
BIG = 1e30
DIAG, UP = 128.0, 129.0
MAGIC = 12582912.0
NTILE = B * N // P
GT = 4
NG = NTILE // GT
assert PAD <= NT - N and NT % STEPS == 0 and NT >= N + PAD and PITCH >= PAD + NT and STEPS % RR == 0 and TB % 2 == 0


def pair(buf, r, lo, hi):
    ring = buf.shape[1]
    r %= ring
    if r == ring - 1:
        return buf[:, ring - 1::-(ring - 1), lo:hi]
    return buf[:, r:r + 2, lo:hi]


def pair_down(buf, r):
    r %= buf.shape[1]
    return buf[:, r:r + 2, W - 1::-1]


def dtw_ffn_kernel(nc, x, ctx_in, w_r, w_k, w_v, mu_r, mu_k, out):
    with ExitStack() as es:
        def sb(name, shape, dt=FP32):
            return es.enter_context(nc.sbuf_tensor(name, shape, dt))

        def sem(name):
            return es.enter_context(nc.semaphore(name))

        d_scr = nc.dram_tensor("d_scratch", (B * N, PITCH), FP32, kind="Internal").ap()
        ch_scr = nc.dram_tensor("choice_scratch", (NBLK, P, TB * (W + 1)), BF16, kind="Internal").ap()
        cnt_scr = nc.dram_tensor("count_scratch", (2 * P, NT), FP32, kind="Internal").ap()

        reg_a = sb("reg_a", [P, KC * B * N])
        reg_b = sb("reg_b", [P, 12480])
        reg_c = sb("reg_c", [P, 18048])
        ident = sb("ident", [P, P])
        identb = sb("identb", [P, P], BF16)
        eps = sb("eps", [P, 1])
        tiny = sb("tiny", [P, 1])
        magic = sb("magic", [P, 2])
        mu = sb("mu", [P, 2, KC])
        omu = sb("omu", [P, 2, KC])
        iota1 = sb("iota1", [P, N])
        bsel = sb("bsel", [P, B])
        bsrow = sb("bsrow", [B, B, P])
        sqj = sb("sqj", [P, C])
        aa = sb("aa", [P, B])
        aaT = sb("aaT", [B, IB])
        bb = sb("bb", [P, NTILE])
        stat = sb("stat", [P, GT, 6])
        mv = sb("mv", [P, 2, GT, 2])
        sd = sb("sd", [P, 2, GT])
        rstd = sb("rstd", [P, 2, GT])
        rrow = sb("rrow", [P, RR, W + 2])
        mrow = sb("mrow", [P, RR, W + 1])
        padm = sb("padm", [P, TB], BF16)
        cmid = sb("cmid", [P, TB])
        path = sb("path", [P, 2, NIB, B])
        tpre = sb("tpre", [P, 2, N], BF16)

        def part(region, at, size, pattern=None, dt=FP32, **dims):
            a = region[:, at:at + size]
            if dt != FP32:
                a = a.bitcast(dt)
            return a.rearrange(pattern, **dims) if pattern else a

        xnT = part(reg_a, 0, KC * B * N, "p (k t) -> p k t", k=KC)
        wT = part(reg_a, 0, 3 * KC * C, "p (m k c) -> p m k c", m=3, k=KC)
        pm = part(reg_a, 6144, N * NIB, "p (a i j) -> p a i j", BF16, a=2, i=NIB)
        cun = part(reg_a, 14336, 2 * N, "p (q i) -> p q i", q=2)
        ctxn = part(reg_b, 0, B * C, "p (b c) -> p b c", b=B)
        ctxT = part(reg_b, 2048, KC * B * IB, "p (k t) -> p k t", k=KC)
        dstage = part(reg_b, 4096, 2 * JT * IB, "p (a g c) -> p a g c", a=2, g=JT)
        drelu = part(reg_b, 6144, JT * IB, "p (g c) -> p g c", g=JT)
        dring = part(reg_b, 7168, 2 * (W + 1) * TB, "p (a w t) -> p a w t", a=2, w=W + 1)
        tring = part(reg_b, 0, STEPS * (W + 1) // 2, "p (t w) -> p t w", BF16, t=STEPS)
        ering = part(reg_b, 2640, STEPS * (W + 2) // 2, "p (t w) -> p t w", BF16, t=STEPS)
        wnat = part(reg_b, 5360, KC * C, "p (a c) -> p a c", a=KC)
        cnt = part(reg_b, 10240, 2 * NT, "p (q t) -> p q t", q=2)
        ctxb = part(reg_b, 0, NIB * C, "p (i c) -> p i c", i=NIB)
        parts = part(reg_b, 4096, 3 * NIB * C // 2, "p (q i c) -> p q i c", BF16, q=3, i=NIB)
        xs = part(reg_c, 0, NTILE * C, "p (n c) -> p n c", n=NTILE)
        up_better = part(reg_c, 0, STEPS * W // 2, "p (t w) -> p t w", BF16, t=STEPS)
        left_worse = part(reg_c, 2176, STEPS * W // 2, "p (t w) -> p t w", BF16, t=STEPS)
        choice = part(reg_c, 4352, STEPS * (W + 1) // 2, "p (t w) -> p t w", BF16, t=STEPS)
        xg = part(reg_c, 0, 2 * GT * C, "p (a q c) -> p a q c", a=2, q=GT)
        xn2 = part(reg_c, 4096, GT * C, "p (q c) -> p q c", q=GT)
        xT = part(reg_c, 6144, KC * (C + 1), "p (k t) -> p k t", k=KC)
        shift = part(reg_c, 8200, 2 * C, "p (a t) -> p a t", a=2)
        xr = part(reg_c, 9224, KC * C, "p (k t) -> p k t", k=KC)
        xk = part(reg_c, 11272, KC * C, "p (k t) -> p k t", k=KC)
        kact = part(reg_c, 13320, KC * C, "p (k t) -> p k t", k=KC)
        sig = part(reg_c, 15368, 2 * C, "p (a t) -> p a t", a=2)
        rv = part(reg_c, 16392, 2 * C, "p (a t) -> p a t", a=2)
        krelu = part(reg_c, 17416, C)

        ps = [es.enter_context(nc.psum_tensor(f"ps{n}", [P, 512], FP32)) for n in range(8)]

        const_ready = sem("const_ready")
        pool_chain = sem("pool_chain")
        lanes_ready = sem("lanes_ready")
        x_loaded = [sem(f"x_loaded{g}") for g in range(NG)]
        choice_ready = sem("choice_ready")
        choice_written = [sem("choice_written0"), sem("choice_written1")]
        choice_loaded = [sem("choice_loaded0"), sem("choice_loaded1")]
        mu_loaded = sem("mu_loaded")
        w_loaded = sem("w_loaded")
        ctx_loaded = sem("ctx_loaded")
        pad_written = sem("pad_written")
        stats_ready = sem("stats_ready")
        sd_ready = sem("sd_ready")
        xn_ready = sem("xn_ready")
        xt_in_psum = sem("xt_in_psum")
        xt_ready = sem("xt_ready")
        bb_ready = sem("bb_ready")
        dve_step = sem("dve_step")
        ctxt_in_psum = sem("ctxt_in_psum")
        ctxt_ready = sem("ctxt_ready")
        aa_ready = sem("aa_ready")
        aat_in_psum = sem("aat_in_psum")
        aat_ready = sem("aat_ready")
        d_in_psum = sem("d_in_psum")
        d_relu_done = sem("d_relu_done")
        d_staged = sem("d_staged")
        d_written = [sem("d_written0"), sem("d_written1")]
        d_loaded = [sem("d_loaded0"), sem("d_loaded1")]
        fwd_block = sem("fwd_block")
        fwd_done = sem("fwd_done")
        bwd_block = sem("bwd_block")
        ring_free = sem("ring_free")
        w_in_psum = sem("w_in_psum")
        w_ready = sem("w_ready")
        cnt_in_psum = sem("cnt_in_psum")
        cnt_taken = sem("cnt_taken")
        cnt_rounded = sem("cnt_rounded")
        cnt_written = sem("cnt_written")
        cun_loaded = sem("cun_loaded")
        path_in_psum = sem("path_in_psum")
        path_ready = sem("path_ready")
        pm_ready = sem("pm_ready")
        ctxb_loaded = sem("ctxb_loaded")
        hi_ready = sem("hi_ready")
        rest_ready = sem("rest_ready")
        mid_ready = sem("mid_ready")
        lo_ready = sem("lo_ready")
        exp_in_psum = sem("exp_in_psum")
        xmid_ready = sem("xmid_ready")
        xg_loaded = [sem("xg_loaded0"), sem("xg_loaded1")]
        stats2_ready = sem("stats2_ready")
        sd2_ready = sem("sd2_ready")
        xn2_ready = sem("xn2_ready")
        t2_in_psum = sem("t2_in_psum")
        t2_ready = sem("t2_ready")
        border_ready = sem("border_ready")
        xk_ready = sem("xk_ready")
        xr_ready = sem("xr_ready")
        k_in_psum = sem("k_in_psum")
        k_relu_done = sem("k_relu_done")
        k_ready = sem("k_ready")
        r_in_psum = sem("r_in_psum")
        sig_ready = sem("sig_ready")
        v_in_psum = sem("v_in_psum")
        rv_ready = sem("rv_ready")
        y_ready = sem("y_ready")
        y_written = [sem("y_written0"), sem("y_written1")]

        x_h = x.rearrange("b (g q p) c -> (b g) p q c", q=GT, p=P)
        out_h = out.rearrange("b (g q p) c -> (b g) p q c", q=GT, p=P)
        ctx_h = ctx_in.rearrange("b (n p) c -> n p b c", p=P)
        ctxb_h = ctx_in.rearrange("b (n p) c -> b p n c", p=P)
        d_h = d_scr.rearrange("(b g p) c -> b p g c", b=B, p=P)

        block = es.enter_context(nc.Block())

        @block.sync
        def _(sp):
            with nc.allow_non_contiguous_dma("mu, one value in each row"):
                for m, h in enumerate((mu_r, mu_k)):
                    sp.dma_start(mu[:, m, :], h.rearrange("(k p) -> p k", p=P)).then_inc(mu_loaded, 16)
            sp.dma_start(ctxn, ctx_h[0]).then_inc(ctx_loaded, 16)
            for g in range(NG):
                sp.dma_start(xs[:, GT * g:GT * g + GT], x_h[g]).then_inc(x_loaded[g], 16)

            def load_ctx(n):
                sp.wait_ge(ctxt_in_psum, B * n)
                sp.wait_ge(aa_ready, B * n)
                sp.dma_start(ctxn, ctx_h[n]).then_inc(ctx_loaded, 16)

            load_ctx(1)
            at = 1
            sp.wait_ge(pad_written, 32)
            for k in range(NBLK):
                last = min(NIB - 1, (TB * k + TB - 1) // IB)
                while at < min(NIB - 1, last + 1):
                    at += 1
                    load_ctx(at)
                for a in range(2):
                    sp.wait_ge(d_written[a], 16 * (B // 2) * (last + 1))
                if k >= 2:
                    sp.wait_ge(fwd_block, k)
                for b in range(B):
                    src = bass.AP(d_scr.tensor, b * N * PITCH + PAD + TB * k,
                                  [[W * PITCH - SKEW, SEG], [PITCH, W], [1, TB]])
                    sp.dma_start(dring[SEG * b:SEG * b + SEG, k % 2, 0:W, :], src).then_inc(d_loaded[k % 2], 16)
                if k >= 2:
                    sp.wait_ge(choice_ready, k + 1)
                    sp.dma_start(ch_scr[k - 2], choice[:, TB * (k % 2):TB * (k % 2) + TB, :]
                                 .rearrange("p t w -> p (t w)")).then_inc(choice_written[k % 2], 16)
            sp.wait_ge(fwd_done, 1)
            for m, h in enumerate((w_r, w_k, w_v)):
                if m:
                    sp.wait_ge(w_in_psum, KC * m)
                sp.dma_start(wnat, h.rearrange("(a p) c -> p a c", p=P)).then_inc(w_loaded, 16)
            for a in range(2):
                sp.wait_ge(choice_written[a], 16 * (NBLK // 2 - 1))
            for k in range(2, NBLK):
                sp.wait_ge(bwd_block, k - 1)
                m = NBLK - 1 - k
                sp.dma_start(choice[:, TB * (m % 2):TB * (m % 2) + TB, :].rearrange("p t w -> p (t w)"),
                             ch_scr[m]).then_inc(choice_loaded[m % 2], 16)
            sp.wait_ge(cnt_rounded, 2 * NBLK)
            for q in range(2):
                sp.dma_start(cnt_scr[q * P:q * P + P, :], cnt[:, q, :]).then_inc(cnt_written, 16)
            sp.wait_ge(cnt_written, 32)
            for q in range(2):
                for b in range(B):
                    src = bass.AP(cnt_scr.tensor, (q * P + SEG * b) * NT, [[NT + SKEW, SEG], [1, N]])
                    sp.dma_start(cun[SEG * b:SEG * b + SEG, q, :], src).then_inc(cun_loaded, 16)
            sp.wait_ge(cnt_in_psum, 2 * NBLK)
            sp.wait_ge(w_in_psum, 3 * KC)
            sp.dma_start(ctxb, ctxb_h[0]).then_inc(ctxb_loaded, 16)
            for g in range(2):
                sp.dma_start(xg[:, g], x_h[g]).then_inc(xg_loaded[g], 16)
            for g in range(NG):
                b = g // 2
                if g % 2 == 0 and b + 1 < B:
                    sp.wait_ge(lo_ready, NIB * (b + 1))
                    sp.dma_start(ctxb, ctxb_h[b + 1]).then_inc(ctxb_loaded, 16)
                sp.wait_ge(y_ready, GT * (g + 1))
                sp.dma_start(out_h[g], xg[:, g % 2]).then_inc(y_written[g % 2], 16)
                if g + 2 < NG:
                    sp.wait_ge(y_written[g % 2], 16 * (g // 2 + 1))
                    sp.dma_start(xg[:, g % 2], x_h[g + 2]).then_inc(xg_loaded[g % 2], 16)
            for a in range(2):
                sp.wait_ge(y_written[a], 16 * NG // 2)

        @block.gpsimd
        def _(pool):
            steps = [0]

            def after(ins):
                steps[0] += 1
                ins.then_inc(pool_chain, 1)
                pool.wait_ge(pool_chain, steps[0])

            after(pool.memset(ident[:, :], 0.0))
            after(pool.affine_select(out=ident[:, :], in_=ident[:, :], compare_op=ALU.not_equal, fill=1.0,
                                     base=0, pattern=[[-1, P]], channel_multiplier=1))
            after(pool.tensor_copy(identb[:, :], ident[:, :]))
            after(pool.memset(bsrow[:, :, :], 0.0))
            after(pool.affine_select(out=bsrow[:, :, :], in_=bsrow[:, :, :], compare_op=ALU.not_equal, fill=1.0,
                                     base=0, pattern=[[-1, B], [0, P]], channel_multiplier=1))
            after(pool.memset(tiny[:, :], 1e-34))
            pool.memset(eps[:, :], 1e-5).then_inc(const_ready, 1)
            zeros = part(reg_b, 7168, W * (NT - N), "p (r c) -> p r c", r=W)
            after(pool.memset(zeros, 0.0))
            rows = d_scr.rearrange("(p r) c -> p r c", p=P)
            pool.dma_start(rows[:, :, 0:PAD], zeros[:, :, 0:PAD]).then_inc(pad_written, 16)
            pool.dma_start(rows[:, :, PAD + N:PAD + NT], zeros).then_inc(pad_written, 16)
            after(pool.memset(magic[:, 0:1], MAGIC))
            after(pool.memset(magic[:, 1:2], -MAGIC))
            after(pool.memset(bsel[:, :], 0.0))
            for b in range(B):
                after(pool.memset(bsel[SEG * b:SEG * b + SEG, b:b + 1], 1.0))
            after(pool.iota(iota1[:, :], pattern=[[1, N]], base=1, channel_multiplier=0,
                            allow_small_or_imprecise_dtypes=True))
            after(pool.memset(padm[:, :], UP))
            for b in range(B):
                q = padm[SEG * b:SEG * b + SEG, :]
                after(pool.affine_select(out=q, in_=q, compare_op=ALU.is_gt, fill=0.0, base=NT - TB - N + 1,
                                         pattern=[[1, TB]], channel_multiplier=-SKEW))
            pool.wait_ge(pad_written, 32)
            after(pool.memset(dring[:, :, W, :], 0.0))
            for b in range(B):
                q = dring[SEG * b:SEG * b + SEG, :, W, :]
                after(pool.affine_select(out=q, in_=q, compare_op=ALU.not_equal, fill=BIG, base=1 - SEG,
                                         pattern=[[0, 2], [0, TB]], channel_multiplier=1))
            pool.wait_ge(xt_in_psum, NTILE)
            pool.wait_ge(bb_ready, NTILE)
            pool.memset(choice[:, :, W:W + 1], 0.0).then_inc(lanes_ready, 1)
            pool.sem_inc(choice_ready, 2)
            for k in range(NBLK - 1):
                rows = slice(TB * (k % 2), TB * (k % 2) + TB)
                pool.wait_ge(fwd_block, k + 2)
                if k >= 2:
                    pool.wait_ge(choice_written[k % 2], 16 * (k // 2))
                after(pool.tensor_scalar(up_better[:, rows, :], up_better[:, rows, :], DIAG, None, ALU.add))
                pool.tensor_tensor(choice[:, rows, 0:W], up_better[:, rows, :], left_worse[:, rows, :],
                                   ALU.mult).then_inc(choice_ready, 1)
            for b in range(B):
                for i in range(NIB):
                    pool.wait_ge(hi_ready, NIB * b + i + 1)
                    pool.tensor_tensor(ctxb[:, i], ctxb[:, i], parts[:, 0, i], ALU.subtract).then_inc(rest_ready, 1)
                for i in range(NIB):
                    pool.wait_ge(mid_ready, NIB * b + i + 1)
                    pool.tensor_tensor(parts[:, 2, i], ctxb[:, i], parts[:, 1, i], ALU.subtract).then_inc(lo_ready, 1)

        @block.scalar
        def _(act):
            act.wait_ge(const_ready, 1)
            for g in range(NG + 1):
                if g < NG:
                    act.wait_ge(stats_ready, g + 1)
                    if g >= 2:
                        act.wait_ge(xn_ready, GT * (g - 1))
                    act.activation(sd[:, g % 2], mv[:, g % 2, :, 1], ACT.Sqrt, bias=eps[:, 0:1]).then_inc(sd_ready, 1)
                for n in range(GT * (g - 1), GT * g) if g else ():
                    act.wait_ge(xn_ready, n + 1)
                    if n:
                        act.wait_ge(bb_ready, n)
                    act.activation(sqj[:, :], xs[:, n], ACT.Square,
                                   accum_out=bb[:, n:n + 1]).then_inc(bb_ready, 1)
                    act.wait_ge(xt_in_psum, n + 1)
                    act.activation(xnT[:, :, P * n:P * n + P], ps[n % 2][:, :].rearrange("p (k t) -> p k t", k=KC),
                                   ACT.Copy).then_inc(xt_ready, 1)
            squares = 0
            act.wait_ge(bb_ready, NTILE)
            for n in range(NIB):
                act.wait_ge(ctx_loaded, 16 * (n + 1))
                if n:
                    act.wait_ge(aat_in_psum, n)
                for b in range(B):
                    if squares:
                        act.wait_ge(aa_ready, squares)
                    act.activation(sqj[:, :], ctxn[:, b], ACT.Square, accum_out=aa[:, b:b + 1]).then_inc(aa_ready, 1)
                    squares += 1
                if n:
                    act.wait_ge(d_in_psum, 2 * B * n)
                for b in range(B):
                    act.wait_ge(ctxt_in_psum, B * n + b + 1)
                    act.activation(ctxT[:, :, IB * b:IB * b + IB],
                                   ps[4 + b % 2][:, :].rearrange("p (k t) -> p k t", k=KC), ACT.Copy)\
                       .then_inc(ctxt_ready, 1)
                act.wait_ge(aat_in_psum, n + 1)
                act.activation(aaT[:, :], ps[6][0:B, 0:IB], ACT.Copy, scale=-0.5).then_inc(aat_ready, 1)
                for b in range(B):
                    o = B * n + b
                    if o:
                        act.wait_ge(d_staged, o)
                    for h in range(2):
                        act.wait_ge(d_in_psum, 2 * o + h + 1)
                        for q in range(4):
                            g = 4 * h + q
                            last = act.activation(drelu[:, g], ps[2 * (b % 2) + h][:, IB * q:IB * q + IB], ACT.Relu,
                                                  bias=bb[:, JT * b + g:JT * b + g + 1], scale=-2.0)
                        last.then_inc(d_relu_done, 1)
                    act.wait_ge(d_relu_done, 2 * (o + 1))
                    if o >= 2:
                        act.wait_ge(d_written[o % 2], 16 * (o // 2))
                    act.activation(dstage[:, o % 2], drelu, ACT.Sqrt, bias=tiny[:, 0:1]).then_inc(d_staged, 1)
                    act.wait_ge(d_staged, o + 1)
                    act.dma_start(d_h[b, :, :, PAD + IB * n:PAD + IB * n + IB], dstage[:, o % 2])\
                       .then_inc(d_written[o % 2], 16)
            for n in range(3 * KC):
                act.wait_ge(w_in_psum, n + 1)
                act.activation(wT[:, n // KC, :, P * (n % KC):P * (n % KC) + P],
                               ps[4 + n % 2][:, :].rearrange("p (k t) -> p k t", k=KC), ACT.Copy).then_inc(w_ready, 1)
            act.wait_ge(lanes_ready, 1)
            for k in range(NBLK):
                lo = NT - TB * (k + 1)
                act.wait_ge(cnt_in_psum, 2 * k + 1)
                act.activation(cnt[:, 0, lo:lo + TB], ps[2 * (k % 2)][:, 0:TB], ACT.Copy).then_inc(cnt_rounded, 1)
                act.wait_ge(cnt_in_psum, 2 * k + 2)
                if k:
                    act.wait_ge(cnt_rounded, 2 * k)
                act.activation(cmid[:, :], ps[2 * (k % 2) + 1][:, 0:TB], ACT.Identity, bias=magic[:, 0:1],
                               scale=1.0 / DIAG).then_inc(cnt_taken, 1)
                act.wait_ge(cnt_taken, k + 1)
                act.activation(cnt[:, 1, lo:lo + TB], cmid[:, :], ACT.Identity, bias=magic[:, 1:2])\
                   .then_inc(cnt_rounded, 1)

            def first_parts(b):
                act.wait_ge(ctxb_loaded, 16 * (b + 1))
                if b:
                    act.wait_ge(exp_in_psum, 2 * GT * b)
                for i in range(NIB):
                    act.activation(parts[:, 0, i], ctxb[:, i], ACT.Copy).then_inc(hi_ready, 1)

            def second_parts(b):
                for i in range(NIB):
                    act.wait_ge(rest_ready, NIB * b + i + 1)
                    act.activation(parts[:, 1, i], ctxb[:, i], ACT.Copy).then_inc(mid_ready, 1)

            def deviation(g):
                act.wait_ge(stats2_ready, g + 1)
                if g >= 2:
                    act.wait_ge(xn2_ready, GT * (g - 1))
                act.activation(sd[:, g % 2], mv[:, g % 2, :, 1], ACT.Sqrt, bias=eps[:, 0:1]).then_inc(sd2_ready, 1)

            act.wait_ge(cun_loaded, 128)
            first_parts(0)
            second_parts(0)
            deviation(0)
            for g in range(NG):
                act.wait_ge(border_ready, g + 1)
                for n in range(GT * g, GT * g + GT):
                    act.wait_ge(t2_in_psum, n + 1)
                    act.activation(xT[:, :, 1 + P * (n % GT):1 + P * (n % GT) + P],
                                   ps[2 + n % 2][:, :].rearrange("p (k t) -> p k t", k=KC), ACT.Copy)\
                       .then_inc(t2_ready, 1)
                if g + 1 < NG:
                    deviation(g + 1)
                more = g % 2 == 0 and g // 2 + 1 < B
                if more:
                    first_parts(g // 2 + 1)
                if g:
                    act.wait_ge(v_in_psum, GT * g)
                for n in range(KC * g, KC * g + KC):
                    act.wait_ge(k_in_psum, n + 1)
                    if n:
                        act.wait_ge(k_ready, n)
                    act.activation(krelu, ps[4 + n % 2][:, :], ACT.Relu).then_inc(k_relu_done, 1)
                    act.wait_ge(k_relu_done, n + 1)
                    act.activation(kact[:, n % KC], krelu, ACT.Square).then_inc(k_ready, 1)
                if more:
                    second_parts(g // 2 + 1)
                for n in range(GT * g, GT * g + GT):
                    act.wait_ge(r_in_psum, n + 1)
                    if n >= 2:
                        act.wait_ge(rv_ready, n - 1)
                    act.activation(sig[:, n % 2], ps[6][:, :], ACT.Sigmoid).then_inc(sig_ready, 1)

        @block.tensor
        def _(pe):
            pe.wait_ge(const_ready, 1)
            for n in range(NTILE):
                pe.wait_ge(xn_ready, n + 1)
                if n >= 2:
                    pe.wait_ge(xt_ready, n - 1)
                for k in range(KC):
                    last = pe.transpose(ps[n % 2][:, P * k:P * k + P], xs[:, n, P * k:P * k + P],
                                        ident[:, :])
                last.then_inc(xt_in_psum, 1)
            pe.wait_ge(xt_ready, NTILE)
            for n in range(NIB):
                pe.wait_ge(ctx_loaded, 16 * (n + 1))
                for b in range(B):
                    if B * n + b >= 2:
                        pe.wait_ge(ctxt_ready, B * n + b - 1)
                    for k in range(KC):
                        last = pe.transpose(ps[4 + b % 2][:, P * k:P * k + P], ctxn[:, b, P * k:P * k + P],
                                            ident[:, :])
                    last.then_inc(ctxt_in_psum, 1)
                pe.wait_ge(aa_ready, B * (n + 1))
                if n:
                    pe.wait_ge(aat_ready, n)
                pe.transpose(ps[6][0:B, 0:IB], aa[:, :], ident[:, :]).then_inc(aat_in_psum, 1)
                pe.wait_ge(ctxt_ready, B * (n + 1))
                pe.wait_ge(aat_ready, n + 1)
                for b in range(B):
                    for h in range(2):
                        o = 2 * (B * n + b) + h
                        if o >= 4:
                            pe.wait_ge(d_relu_done, o - 3)
                        for q in range(4):
                            dst = ps[2 * (b % 2) + h][:, IB * q:IB * q + IB]
                            j = N * b + P * (4 * h + q)
                            for k in range(KC):
                                pe.matmul(dst, xnT[:, k, j:j + P], ctxT[:, k, IB * b:IB * b + IB],
                                          start=(k == 0), stop=False)
                            last = pe.matmul(dst, bsrow[:, b, :], aaT[:, :], start=False, stop=True)
                        last.then_inc(d_in_psum, 1)
            for n in range(3 * KC):
                pe.wait_ge(w_loaded, 16 * (n // KC + 1))
                if n >= 2:
                    pe.wait_ge(w_ready, n - 1)
                for k in range(KC):
                    last = pe.transpose(ps[4 + n % 2][:, P * k:P * k + P], wnat[:, n % KC, P * k:P * k + P],
                                        ident[:, :])
                last.then_inc(w_in_psum, 1)
            pe.wait_ge(d_relu_done, 2 * B * NIB)
            pe.sem_inc(ring_free, 1)
            for k in range(NBLK):
                pe.wait_ge(bwd_block, k + 1)
                if k >= 2:
                    pe.wait_ge(cnt_rounded, 2 * (k - 1))
                at = TB * (k % 2)
                for q, (ring, first) in enumerate(((tring, 0), (ering, 1))):
                    for j in range(W):
                        rows = ring[:, at + TB - 1:at - 1 if at else None:-1, first + j]
                        last = pe.matmul(ps[2 * (k % 2) + q][:, 0:TB], identb[:, :], rows,
                                         start=(j == 0), stop=(j == W - 1))
                    last.then_inc(cnt_in_psum, 1)
                pe.wait_ge(cnt_in_psum, 2 * (k + 1))
                pe.sem_inc(ring_free, 1)
            pe.wait_ge(lanes_ready, 1)
            pe.wait_ge(w_ready, 3 * KC)
            pe.wait_ge(cun_loaded, 128)
            for q in range(2):
                for i in range(NIB):
                    last = pe.matmul(ps[4][:, (NIB * q + i) * B:(NIB * q + i + 1) * B],
                                     cun[:, q, P * i:P * i + P], bsel[:, :], start=True, stop=True)
            last.then_inc(path_in_psum, 1)

            def expand(g):
                b = g // 2
                pe.wait_ge(pm_ready, NIB * (b + 1))
                pe.wait_ge(lo_ready, NIB * (b + 1))
                for n in range(GT * g, GT * g + GT):
                    if n >= 2:
                        pe.wait_ge(xmid_ready, n - 1)
                    j = P * (n % JT)
                    for q in range(3):
                        for i in range(NIB):
                            last = pe.matmul(ps[n % 2][:, :], pm[:, b % 2, i, j:j + P], parts[:, q, i],
                                             start=(q == i == 0), stop=(q == 2 and i == NIB - 1))
                    last.then_inc(exp_in_psum, 1)

            pe.wait_ge(path_ready, 1)
            expand(0)
            for g in range(NG):
                for n in range(GT * g, GT * g + GT):
                    pe.wait_ge(xn2_ready, n + 1)
                    if n >= 2:
                        pe.wait_ge(t2_ready, n - 1)
                    for k in range(KC):
                        last = pe.transpose(ps[2 + n % 2][:, P * k:P * k + P], xn2[:, n % GT, P * k:P * k + P],
                                            ident[:, :])
                    last.then_inc(t2_in_psum, 1)
                if g + 1 < NG:
                    expand(g + 1)
                pe.wait_ge(xk_ready, g + 1)
                for n in range(KC * g, KC * g + KC):
                    if n >= 2:
                        pe.wait_ge(k_relu_done, n - 1)
                    m = P * (n % KC)
                    for c in range(KC):
                        last = pe.matmul(ps[4 + n % 2][:, :], wT[:, 1, c, m:m + P], xk[:, c],
                                         start=(c == 0), stop=(c == KC - 1))
                    last.then_inc(k_in_psum, 1)
                pe.wait_ge(xr_ready, g + 1)
                for n in range(GT * g, GT * g + GT):
                    t = P * (n % GT)
                    if n:
                        pe.wait_ge(sig_ready, n)
                    for c in range(KC):
                        last = pe.matmul(ps[6][:, :], xr[:, c, t:t + P], wT[:, 0, c, :],
                                         start=(c == 0), stop=(c == KC - 1))
                    last.then_inc(r_in_psum, 1)
                    pe.wait_ge(k_ready, KC * (g + 1))
                    if n:
                        pe.wait_ge(rv_ready, n)
                    for c in range(KC):
                        last = pe.matmul(ps[7][:, :], kact[:, c, t:t + P], wT[:, 2, c, :],
                                         start=(c == 0), stop=(c == KC - 1))
                    last.then_inc(v_in_psum, 1)

        @block.vector
        def _(dve):
            steps = [0]

            def after(ins):
                steps[0] += 1
                ins.then_inc(dve_step, 1)
                dve.wait_ge(dve_step, steps[0])

            def stats(src, g, ready):
                for q in range(GT):
                    last = dve.bn_stats(stat[:, q], src[:, q])
                after(last)
                for q in range(GT):
                    last = dve.bn_aggr(mv[:, g % 2, q], stat[:, q])
                steps[0] += 1
                last.then_inc(dve_step, 1)
                dve.wait_ge(dve_step, steps[0])
                dve.sem_inc(ready, 1)

            def normalise(dst, src, g, sd_sem, ready):
                dve.wait_ge(sd_sem, g + 1)
                after(dve.reciprocal(rstd[:, g % 2], sd[:, g % 2]))
                for q in range(GT):
                    dve.tensor_scalar(dst[:, q], src[:, q], mv[:, g % 2, q, 0:1], rstd[:, g % 2, q:q + 1],
                                      ALU.subtract, ALU.mult).then_inc(ready, 1)

            dve.wait_ge(const_ready, 1)
            dve.wait_ge(mu_loaded, 32)
            after(dve.tensor_scalar(omu[:, :, :], mu[:, :, :], -1.0, 1.0, ALU.mult, ALU.add))
            for g in range(NG + 1):
                if g < NG:
                    dve.wait_ge(x_loaded[g], 16)
                    stats(xs[:, GT * g:GT * g + GT], g, stats_ready)
                if g:
                    tiles = xs[:, GT * (g - 1):GT * g]
                    normalise(tiles, tiles, g - 1, sd_ready, xn_ready)

            after(dve.memset(rrow[:, :, :], BIG))
            after(dve.memset(mrow[:, :, :], BIG))
            for b in range(B):
                after(dve.memset(rrow[SEG * b:SEG * b + 1, RR - 1, 0:1], 0.0))
            dve.wait_ge(lanes_ready, 1)
            dve.sem_clear(dve_step)
            with dve.Fori(0, NT // STEPS) as it:
                for t in range(STEPS):
                    r = t % RR
                    if t % TB == 0:
                        dve.wait_ge(d_loaded[t // TB], it * (16 * B) + 16 * B)
                    if t:
                        dve.wait_ge(dve_step, 4 * t - 1)
                    if t % TB == 2:
                        dve.wait_ge(choice_ready, it * 2 + t // TB + 1)
                    if t % TB == 3:
                        dve.sem_inc(fwd_block, 1)
                    dve.tensor_tensor(mrow[:, r, 0:W], rrow[:, (r - 1) % RR, 1:W + 1], rrow[:, (r - 1) % RR, 0:W],
                                      ALU.min).then_inc(dve_step, 1)
                    dve.stream_shuffle(rrow[:, (r + 1) % RR, 0:1], rrow[:, (r - 1) % RR, W + 1:W + 2],
                                       [SEG - 1] + list(range(SEG - 1))).then_inc(dve_step, 1)
                    dve.wait_ge(dve_step, 4 * t + 1)
                    dve.tensor_tensor_scan(rrow[:, r, 1:W + 2], mrow[:, r, :], dring[:, t // TB, :, t % TB],
                                           rrow[:, r, 0:1], ALU.min, ALU.add).then_inc(dve_step, 1)
                    if t % 2 == 0:
                        dve.tensor_tensor(pair_down(up_better, t - 2), pair(rrow, r - 3, 1, W + 1),
                                          pair(rrow, r - 3, 0, W), ALU.is_lt).then_inc(dve_step, 1)
                    else:
                        dve.tensor_tensor(pair_down(left_worse, t - 3), pair(mrow, r - 3, 0, W),
                                          pair(rrow, r - 3, 0, W), ALU.is_le).then_inc(dve_step, 1)
                dve.wait_ge(dve_step, 4 * STEPS)
                dve.sem_clear(dve_step)
            dve.wait_ge(choice_written[1], 16 * (NBLK // 2 - 1))
            dve.scalar_tensor_tensor(choice[:, TB:STEPS, 0:W], up_better[:, TB:STEPS, :], DIAG,
                                     left_worse[:, TB:STEPS, :], ALU.add, ALU.mult).then_inc(dve_step, 1)
            for a in range(2):
                dve.wait_ge(d_written[a], 16 * B * NIB // 2)
            dve.memset(tring[:, 0:1, 0:W], 1.0).then_inc(dve_step, 1)
            dve.memset(tring[:, :, W:W + 1], 1.0).then_inc(dve_step, 1)
            dve.memset(ering[:, 0:SKEW, :], 0.0).then_inc(dve_step, 1)
            dve.memset(ering[:, STEPS - 1:STEPS, :], 0.0).then_inc(dve_step, 1)
            dve.wait_ge(dve_step, 5)
            dve.tensor_tensor(choice[:, TB:STEPS, 0:W], choice[:, TB:STEPS, 0:W],
                              padm[:, :].unsqueeze(2).broadcast_to([P, TB, W]), ALU.max).then_inc(dve_step, 1)
            for b in range(B):
                dve.memset(tring[SEG * b:SEG * b + 1, :, W:W + 1], 0.0).then_inc(dve_step, 1)
            dve.wait_ge(dve_step, 6 + B)
            dve.wait_ge(choice_ready, NBLK + 1)
            for a in range(2):
                dve.sem_inc(choice_loaded[a], 16)
            dve.sem_inc(fwd_done, 1)
            dve.sem_clear(dve_step)

            with dve.Fori(0, NT // STEPS) as it:
                for u in range(STEPS):
                    if u:
                        dve.wait_ge(dve_step, 3 * u)
                    if u % TB == 0:
                        dve.wait_ge(choice_loaded[(u // TB + 1) % 2], it * 16 + 16)
                        if u:
                            dve.sem_inc(bwd_block, 1)
                    if u % TB == TB - 3:
                        dve.wait_ge(ring_free, it * 2 + (u // TB + 1))
                    dve.tensor_tensor_scan(ering[:, u, 1:W + 2], choice[:, STEPS - 1 - u, :], tring[:, u, :],
                                           ering[:, u, 0:1], ALU.max, ALU.mult).then_inc(dve_step, 1)
                    dve.stream_shuffle(ering[:, (u + 1) % STEPS, 0:1], ering[:, (u - 1) % STEPS, W + 1:W + 2],
                                       list(range(1, SEG)) + [0]).then_inc(dve_step, 1)
                    dve.wait_ge(dve_step, 3 * u + 1)
                    dve.scalar_tensor_tensor(tring[:, (u + 1) % STEPS, 0:W], ering[:, u, 1:W + 1], DIAG,
                                             ering[:, u, 0:W], ALU.is_gt, ALU.logical_or).then_inc(dve_step, 1)
                dve.wait_ge(dve_step, 3 * STEPS)
                dve.sem_inc(bwd_block, 1)
                dve.sem_clear(dve_step)
            steps[0] = 0
            dve.wait_ge(path_in_psum, 1)
            after(dve.tensor_copy(path[:, :, :, :].rearrange("p q i b -> p (q i b)"), ps[4][:, 0:2 * NIB * B]))
            dve.sem_inc(path_ready, 1)

            def build(b):
                if b >= 2:
                    dve.wait_ge(exp_in_psum, 2 * GT * (b - 1))
                for i in range(NIB):
                    if NIB * b + i >= 2:
                        dve.wait_ge(pm_ready, NIB * b + i - 1)
                    after(dve.tensor_scalar(tpre[:, i % 2], iota1[:, :], path[:, 1, i, b:b + 1], None, ALU.is_ge))
                    dve.scalar_tensor_tensor(pm[:, b % 2, i], iota1[:, :], path[:, 0, i, b:b + 1], tpre[:, i % 2],
                                             ALU.is_le, ALU.mult).then_inc(pm_ready, 1)

            def mid(g):
                dve.wait_ge(xg_loaded[g % 2], 16 * (g // 2 + 1))
                for n in range(GT * g, GT * g + GT):
                    dve.wait_ge(exp_in_psum, n + 1)
                    dve.tensor_tensor(xg[:, g % 2, n % GT], xg[:, g % 2, n % GT], ps[n % 2][:, :], ALU.add)\
                       .then_inc(xmid_ready, 1)
                dve.wait_ge(xmid_ready, GT * (g + 1))
                stats(xg[:, g % 2], g, stats2_ready)
                if g:
                    dve.wait_ge(t2_in_psum, GT * g)
                normalise(xn2, xg[:, g % 2], g, sd2_ready, xn2_ready)

            def border(g):
                if g % 2 == 0:
                    after(dve.memset(xT[:, :, 0:1], 0.0))
                else:
                    after(dve.tensor_copy(xT[:, :, 0:1], xT[:, :, C:C + 1]))
                dve.sem_inc(border_ready, 1)

            build(0)
            mid(0)
            border(0)
            for g in range(NG):
                dve.wait_ge(t2_ready, GT * (g + 1))
                for m, dst, used, ready in ((1, xk, k_in_psum, xk_ready), (0, xr, r_in_psum, xr_ready)):
                    if g:
                        dve.wait_ge(used, GT * g)
                    for c in range(KC):
                        after(dve.tensor_scalar(shift[:, c % 2], xT[:, c, 0:C], omu[:, m, c:c + 1], None, ALU.mult))
                        after(dve.scalar_tensor_tensor(dst[:, c], xT[:, c, 1:C + 1], mu[:, m, c:c + 1], shift[:, c % 2],
                                                       ALU.mult, ALU.add))
                    dve.sem_inc(ready, 1)
                if g + 1 < NG:
                    border(g + 1)
                    mid(g + 1)
                if g % 2 == 0 and g // 2 + 1 < B:
                    build(g // 2 + 1)
                for n in range(GT * g, GT * g + GT):
                    dve.wait_ge(sig_ready, n + 1)
                    dve.wait_ge(v_in_psum, n + 1)
                    dve.tensor_tensor(rv[:, n % 2], ps[7][:, :], sig[:, n % 2], ALU.mult).then_inc(rv_ready, 1)
                    dve.wait_ge(rv_ready, n + 1)
                    dve.tensor_tensor(xg[:, g % 2, n % GT], xg[:, g % 2, n % GT], rv[:, n % 2], ALU.add)\
                       .then_inc(y_ready, 1)


_INS = ["x", "ctx_1024", "L0_ffn_W_r", "L0_ffn_W_k", "L0_ffn_W_v", "L0_ffn_mu_r", "L0_ffn_mu_k"]


def kernel(**inputs):
    import numpy as _np
    import concourse.bacc as _bacc
    from concourse import mybir as _mybir
    from concourse.bass_utils import run_bass_kernel_spmd as _run

    nc = _bacc.Bacc("TRN2", target_bir_lowering=False, num_devices=1)
    arrays, args = {}, []
    for name in _INS:
        a = _np.ascontiguousarray(inputs[name])
        arrays[f"in_{name}"] = a
        args.append(nc.dram_tensor(f"in_{name}", a.shape, _mybir.dt.from_np(a.dtype), kind="ExternalInput").ap())
    out = nc.dram_tensor("out_y", (4, 1024, 512), _mybir.dt.float32, kind="ExternalOutput").ap()
    dtw_ffn_kernel(nc, *args, out)
    return _run(nc, [arrays], core_ids=[0]).results[0]["out_y"]
```

```python
import concourse.bass as bass
from concourse import mybir
from contextlib import ExitStack

FP32 = mybir.dt.float32
BF16 = mybir.dt.bfloat16
FP32R = mybir.dt.float32r
ALU = mybir.AluOpType
ACT = mybir.ActivationFunctionType

B, N, C = 4, 1024, 512
P = 128
KC = C // P
SEG, W = P // B, N * B // P
SKEW = 2
PAD = SKEW * (SEG - 1)
TB = 68
STEPS = 2 * TB
NT = 1088
NBLK = NT // TB
PITCH = 1152
IB = 128
D_BLOCKS = [(i, min(IB, N - i)) for i in range(0, N, IB)]
NIB = len(D_BLOCKS)
JT = N // P
RR = 8
BIG = 1e30
DIAG, UP = 128.0, 129.0
MAGIC = 12582912.0
NTILE = B * N // P
GT = 4
NG = NTILE // GT
FT = 2
FW = FT * P
FG = NTILE // FT
GB = JT // FT
assert PAD <= NT - N and NT % STEPS == 0 and NT >= N + PAD and PITCH >= PAD + NT and STEPS % RR == 0 and TB % 2 == 0


UC = 2
STAGES = tuple(range(N // P - UC, -1, -UC))
UNITS = [(c, b) for c in STAGES for b in range(B)]
EARLY = len(UNITS) - B
UR = 3
AHEAD = 3
BUILD_AFTER = {b - 1: b for b in range(1, UR)}
BUILD_AFTER[GB - 1] = B - 1
assert UR == B - 1
STAGE_BLOCK = [(NT - 1 - P * c) // TB for c in STAGES]
UNITS_PER_BLOCK = {5: 1, 6: 1, 7: 1, 8: 1, 9: 1, 10: 1, 11: 2, 12: 1, 13: 2, 14: 1}
UNITS_AT, _next = {}, 0
for _k in range(NBLK):
    UNITS_AT[_k] = list(range(_next, _next + UNITS_PER_BLOCK.get(_k, 0)))
    _next += len(UNITS_AT[_k])
assert all(_k >= STAGE_BLOCK[u // B] for _k in UNITS_AT for u in UNITS_AT[_k])
assert sum(UNITS_AT.values(), []) == list(range(EARLY)) and not UNITS_AT[NBLK - 1]


def pair(buf, r, lo, hi):
    ring = buf.shape[1]
    r %= ring
    if r == ring - 1:
        return buf[:, ring - 1::-(ring - 1), lo:hi]
    return buf[:, r:r + 2, lo:hi]


def pair_down(buf, r):
    r %= buf.shape[1]
    return buf[:, r:r + 2, W - 1::-1]


def dtw_ffn_kernel(nc, x, ctx_in, w_r, w_k, w_v, mu_r, mu_k, out):
    with ExitStack() as es:
        def sb(name, shape, dt=FP32):
            return es.enter_context(nc.sbuf_tensor(name, shape, dt))

        def sem(name):
            return es.enter_context(nc.semaphore(name))

        d_scr = nc.dram_tensor("d_scratch", (B * N, PITCH), FP32, kind="Internal").ap()
        ch_scr = nc.dram_tensor("choice_scratch", (NBLK, P, TB * (W + 1)), BF16, kind="Internal").ap()
        cnt_scr = nc.dram_tensor("count_scratch", (2 * P, NT), FP32, kind="Internal").ap()

        reg_a = sb("reg_a", [P, KC * B * N])
        with nc.sbuf_tensor("reg_b", [P, 12240], FP32) as reg_b, nc.sbuf_tensor("reg_c", [P, 17920], FP32) as reg_c:
            pass

        def operand(name, words):
            return sb(name, [P, words], FP32R)

        sb("below_xk", [P, 2064])
        xk = [operand("xk_high", KC * FW), operand("xk_low", KC * FW)]
        sb("above_xk", [P, 448])
        wT = [operand("w_high_part", 3 * KC * C)]
        kact = [operand("kact_low", KC * FW)]
        sb("above_kact", [P, 512 + 3072])
        xr = [operand("xr_high", KC * FW), operand("xr_low", KC * FW)]
        kact.insert(0, operand("kact_high", KC * FW))
        sb("above_kact_high", [P, 5632])
        wT.append(operand("w_low_part", 3 * KC * C))
        xk, kact, xr = ([t.rearrange("p (k t) -> p k t", k=KC) for t in x] for x in (xk, kact, xr))
        wT = [t.rearrange("p (m k c) -> p m k c", m=3, k=KC) for t in wT]
        ident = sb("ident", [P, P])
        identb = sb("identb", [P, P], BF16)
        eps = sb("eps", [P, 1])
        tiny = sb("tiny", [P, 1])
        one = sb("one", [P, 1])
        magic = sb("magic", [P, 2])
        mu = sb("mu", [P, 2, KC])
        omu = sb("omu", [P, 2, KC])
        iota1 = sb("iota1", [P, N])
        bsel = sb("bsel", [P, B])
        work = sb("work", [P, 2 * C])
        aa = sb("aa", [P, B])
        aaT = sb("aaT", [B, 2, IB])
        bb = sb("bb", [P, NTILE])
        stat = sb("stat", [P, GT, 6])
        mv = sb("mv", [P, 2, GT, 2])
        sd = sb("sd", [P, 2, GT])
        rstd = sb("rstd", [P, 2, GT])
        rrow = sb("rrow", [P, RR, W + 2])
        mrow = sb("mrow", [P, RR, W + 1])
        padm = sb("padm", [P, TB], BF16)
        cmid = sb("cmid", [P, TB])
        cnt = sb("cnt", [P, 2, 2, TB])
        path = sb("path", [P, 2, UC, B])
        nbsel = sb("nbsel", [P, B])
        tpre = sb("tpre", [P, 2, N], BF16)
        etmp = sb("etmp", [P, 4, C])

        def part(region, at, size, pattern=None, dt=FP32, **dims):
            a = region[:, at:at + size]
            if dt != FP32:
                a = a.bitcast(dt)
            return a.rearrange(pattern, **dims) if pattern else a

        xnT = part(reg_a, 0, KC * B * N, "p (k t) -> p k t", k=KC)
        acc = part(reg_a, 0, NTILE * C, "p (n c) -> p n c", n=NTILE)
        ctxn = part(reg_b, 0, B * C, "p (b c) -> p b c", b=B)
        ctxT = [part(reg_b, 2048, KC * B * IB, "p (k t) -> p k t", k=KC), etmp]
        dstage = part(reg_b, 4096, 2 * JT * IB, "p (a g c) -> p a g c", a=2, g=JT)
        drelu = part(reg_b, 6144, JT * IB, "p (g c) -> p g c", g=JT)
        dring = part(reg_b, 7168, 2 * (W + 1) * TB, "p (a w t) -> p a w t", a=2, w=W + 1)
        tring = part(reg_b, 0, STEPS * (W + 1) // 2, "p (t w) -> p t w", BF16, t=STEPS)
        ering = part(reg_b, 2244, STEPS * (W + 2) // 2, "p (t w) -> p t w", BF16, t=STEPS)
        cun = part(reg_b, 10704, 2 * UC * P, "p (q i) -> p q i", q=2)
        xn2 = part(reg_b, 0, FT * C, "p (q c) -> p q c", q=FT)
        xT = part(reg_b, 1024, KC * (FW + 1), "p (k t) -> p k t", k=KC)
        xs = part(reg_c, 0, NTILE * C, "p (n c) -> p n c", n=NTILE)
        up_better = part(reg_c, 0, STEPS * W // 2, "p (t w) -> p t w", BF16, t=STEPS)
        left_worse = part(reg_c, 2176, STEPS * W // 2, "p (t w) -> p t w", BF16, t=STEPS)
        choice = part(reg_c, 4352, STEPS * (W + 1) // 2, "p (t w) -> p t w", BF16, t=STEPS)
        pm = part(reg_c, 0, UC * UR * N // 2, "p (i j) -> p i j", BF16, i=UC * UR)
        wnat = part(reg_c, 6656, KC * C, "p (a c) -> p a c", a=KC)
        parts = part(reg_c, 6656, UC * UR * 3 * C // 2, "p (i q c) -> p i q c", BF16, i=UC * UR, q=3)
        wfull = part(reg_c, 3072, 2 * C, "p (a c) -> p a c", a=2)
        ctxb = [part(region, at, UC * C, "p (i c) -> p i c", i=UC) for region, at in ((reg_b, 11216), (reg_c, 3072))]
        sig = [part(reg_b, 11728, C), part(reg_c, 6144, C)]
        sqj = work[:, 0:C]
        bsrow = part(work[0:B, :], C, B * P, "p (b t) -> p b t", b=B)
        dist = work[:, :]
        krelu = [part(reg_c, 11264, C), work[:, 0:C]]
        mix = etmp[:, 0:2, :].rearrange("p a (k t) -> p (a k) t", t=FW)

        def slots(u):
            return range(UC * (u % UR), UC * (u % UR) + UC)

        def ctx_rows(u):
            return ctxb[u % 2] if u < len(UNITS) - 1 else etmp[:, 2:4]

        ps = [es.enter_context(nc.psum_tensor(f"ps{n}", [P, 512], FP32)) for n in range(8)]

        EBANK = (2, 3, 6, 7)

        const_ready = sem("const_ready")
        pool_chain = sem("pool_chain")
        lanes_ready = sem("lanes_ready")
        x_loaded = [sem(f"x_loaded{g}") for g in range(NG)]
        choice_ready = sem("choice_ready")
        choice_written = [sem("choice_written0"), sem("choice_written1")]
        choice_loaded = [sem("choice_loaded0"), sem("choice_loaded1")]
        mu_loaded = sem("mu_loaded")
        w_loaded = sem("w_loaded")
        ctx_loaded = sem("ctx_loaded")
        pad_written = sem("pad_written")
        stats_ready = sem("stats_ready")
        sd_ready = sem("sd_ready")
        xn_ready = sem("xn_ready")
        xt_in_psum = sem("xt_in_psum")
        xt_ready = sem("xt_ready")
        bb_ready = sem("bb_ready")
        dve_step = sem("dve_step")
        ctxt_in_psum = sem("ctxt_in_psum")
        ctxt_ready = sem("ctxt_ready")
        aa_ready = sem("aa_ready")
        aat_in_psum = sem("aat_in_psum")
        aat_ready = sem("aat_ready")
        d_in_psum = sem("d_in_psum")
        d_relu_done = sem("d_relu_done")
        d_staged = sem("d_staged")
        d_written = [sem("d_written0"), sem("d_written1")]
        d_loaded = [sem("d_loaded0"), sem("d_loaded1")]
        fwd_block = sem("fwd_block")
        fwd_done = sem("fwd_done")
        bwd_block = sem("bwd_block")
        ring_free = sem("ring_free")
        w_in_psum = sem("w_in_psum")
        w_taken = sem("w_taken")
        w_high = sem("w_high")
        w_split = sem("w_split")
        cnt_in_psum = sem("cnt_in_psum")
        cnt_taken = sem("cnt_taken")
        cnt_rounded = sem("cnt_rounded")
        cnt_written = [sem("cnt_written0"), sem("cnt_written1")]
        dist_step = sem("dist_step")
        early_in_psum = sem("early_in_psum")
        early_taken = sem("early_taken")
        early_added = sem("early_added")
        cun_loaded = sem("cun_loaded")
        path_in_psum = sem("path_in_psum")
        path_ready = sem("path_ready")
        pm_ready = sem("pm_ready")
        late_pm_ready = sem("late_pm_ready")
        ctxb_loaded = [sem("ctxb_loaded0"), sem("ctxb_loaded1")]
        hi_ready = sem("hi_ready")
        rest_ready = sem("rest_ready")
        mid_ready = sem("mid_ready")
        lo_ready = sem("lo_ready")
        exp_in_psum = sem("exp_in_psum")
        xmid_ready = sem("xmid_ready")
        stats2_ready = sem("stats2_ready")
        sd2_ready = sem("sd2_ready")
        xn2_ready = sem("xn2_ready")
        t2_in_psum = sem("t2_in_psum")
        t2_ready = sem("t2_ready")
        border_ready = sem("border_ready")
        mix_half = sem("mix_half")
        mix_ready = sem("mix_ready")
        mix_high = sem("mix_high")
        mix_split = sem("mix_split")
        k_in_psum = sem("k_in_psum")
        k_relu_done = sem("k_relu_done")
        k_squared = sem("k_squared")
        k_high = sem("k_high")
        k_ready = sem("k_ready")
        r_in_psum = sem("r_in_psum")
        sig_ready = sem("sig_ready")
        v_in_psum = sem("v_in_psum")
        rv_ready = sem("rv_ready")
        y_ready = sem("y_ready")
        y_written = sem("y_written")

        x_h = x.rearrange("b (g q p) c -> (b g) p q c", q=GT, p=P)
        out_h = out.rearrange("b (g q p) c -> (b g) p q c", q=FT, p=P)
        ctx_h = [ctx_in[:, i:i + rows, :].rearrange("b p c -> p b c") for i, rows in D_BLOCKS]
        ctxb_h = ctx_in.rearrange("b (n p) c -> b p n c", p=P)
        cnt_h = cnt_scr.rearrange("(q p) t -> p q t", q=2)
        d_h = d_scr.rearrange("(b g p) c -> b p g c", b=B, p=P)

        block = es.enter_context(nc.Block())

        @block.sync
        def _(sp):
            with nc.allow_non_contiguous_dma("mu, one value in each row"):
                for m, h in enumerate((mu_r, mu_k)):
                    sp.dma_start(mu[:, m, :], h.rearrange("(k p) -> p k", p=P)).then_inc(mu_loaded, 16)
            sp.dma_start(ctxn[0:D_BLOCKS[0][1]], ctx_h[0]).then_inc(ctx_loaded, 16)
            for g in range(NG):
                sp.dma_start(xs[:, GT * g:GT * g + GT], x_h[g]).then_inc(x_loaded[g], 16)

            def load_ctx(n):
                sp.wait_ge(ctxt_in_psum, B * n)
                sp.wait_ge(aa_ready, B * n)
                sp.dma_start(ctxn[0:D_BLOCKS[n][1]], ctx_h[n]).then_inc(ctx_loaded, 16)

            load_ctx(1)
            at = 1
            sp.wait_ge(pad_written, 32)
            for k in range(NBLK):
                last = max(n for n in range(NIB) if D_BLOCKS[n][0] < TB * k + TB)
                while at < min(NIB - 1, last + 1):
                    at += 1
                    load_ctx(at)
                if k >= 2:
                    sp.wait_ge(fwd_block, k)
                for b in range(B):
                    sp.wait_ge(d_written[b % 2], 16 * ((B * last + b) // 2 + 1))
                    src = bass.AP(d_scr.tensor, b * N * PITCH + PAD + TB * k,
                                  [[W * PITCH - SKEW, SEG], [PITCH, W], [1, TB]])
                    sp.dma_start(dring[SEG * b:SEG * b + SEG, k % 2, 0:W, :], src).then_inc(d_loaded[k % 2], 16)
                if k >= 2:
                    sp.wait_ge(choice_ready, k + 1)
                    sp.dma_start(ch_scr[k - 2], choice[:, TB * (k % 2):TB * (k % 2) + TB, :]
                                 .rearrange("p t w -> p (t w)")).then_inc(choice_written[k % 2], 16)
            sp.wait_ge(fwd_done, 1)
            for m, h in enumerate((w_r, w_k, w_v)):
                if m:
                    sp.wait_ge(w_in_psum, KC * m)
                sp.dma_start(wnat, h.rearrange("(a p) c -> p a c", p=P)).then_inc(w_loaded, 16)
            for g in range(NG):
                sp.dma_start(acc[:, GT * g:GT * g + GT], x_h[g]).then_inc(x_loaded[g], 16)

            def load_unit(u):
                c, b = UNITS[u]
                if u >= 2:
                    sp.wait_ge(lo_ready, UC * (u - 1))
                if u == len(UNITS) - 1:
                    sp.wait_ge(early_added, JT * EARLY)
                sp.dma_start(ctx_rows(u), ctxb_h[b, :, c:c + UC]).then_inc(ctxb_loaded[u % 2], 16)

            for a in range(2):
                sp.wait_ge(choice_written[a], 16 * (NBLK // 2 - 1))
            for k in range(NBLK):
                if k + 2 < NBLK:
                    sp.wait_ge(bwd_block, k + 1)
                    m = NBLK - 3 - k
                    sp.dma_start(choice[:, TB * (m % 2):TB * (m % 2) + TB, :].rearrange("p t w -> p (t w)"),
                                 ch_scr[m]).then_inc(choice_loaded[m % 2], 16)
                if k == 0:
                    sp.wait_ge(w_split, 3 * KC)
                    for u in range(AHEAD + 1):
                        load_unit(u)
                sp.wait_ge(cnt_rounded, 2 * (k + 1))
                sp.dma_start(cnt_h[:, :, NT - TB * (k + 1):NT - TB * k], cnt[:, k % 2]).then_inc(cnt_written[k % 2], 16)
                if k in STAGE_BLOCK:
                    stage = STAGE_BLOCK.index(k)
                    sp.wait_ge(cnt_written[0], 16 * (k // 2 + 1))
                    sp.wait_ge(cnt_written[1], 16 * ((k + 1) // 2))
                    if stage:
                        sp.wait_ge(path_in_psum, stage)
                    for b in range(B):
                        src = bass.AP(cnt_scr.tensor, SEG * b * NT + P * STAGES[stage],
                                      [[NT + SKEW, SEG], [P * NT, 2], [1, P * UC]])
                        sp.dma_start(cun[SEG * b:SEG * b + SEG], src).then_inc(cun_loaded, 16)
                for u in UNITS_AT[k]:
                    load_unit(u + AHEAD + 1)
            for g in range(FG):
                sp.wait_ge(y_ready, FT * (g + 1))
                sp.dma_start(out_h[g], acc[:, FT * g:FT * g + FT]).then_inc(y_written, 16)
            sp.wait_ge(y_written, 16 * FG)

        @block.gpsimd
        def _(pool):
            steps = [0]

            def after(ins):
                steps[0] += 1
                ins.then_inc(pool_chain, 1)
                pool.wait_ge(pool_chain, steps[0])

            after(pool.memset(ident[:, :], 0.0))
            after(pool.affine_select(out=ident[:, :], in_=ident[:, :], compare_op=ALU.not_equal, fill=1.0,
                                     base=0, pattern=[[-1, P]], channel_multiplier=1))
            after(pool.tensor_copy(identb[:, :], ident[:, :]))
            after(pool.memset(nbsel[:, :], 0.0))
            for b in range(B):
                after(pool.memset(nbsel[SEG * b:SEG * b + SEG, b:b + 1], -1.0))
            after(pool.memset(bsrow, 0.0))
            after(pool.affine_select(out=bsrow, in_=bsrow, compare_op=ALU.not_equal, fill=1.0,
                                     base=0, pattern=[[-1, B], [0, P]], channel_multiplier=1))
            after(pool.memset(tiny[:, :], 1e-34))
            after(pool.memset(one[:, :], 1.0))
            pool.memset(eps[:, :], 1e-5).then_inc(const_ready, 1)
            zeros = part(reg_b, 7168, W * (NT - N), "p (r c) -> p r c", r=W)
            after(pool.memset(zeros, 0.0))
            rows = d_scr.rearrange("(p r) c -> p r c", p=P)
            pool.dma_start(rows[:, :, 0:PAD], zeros[:, :, 0:PAD]).then_inc(pad_written, 16)
            pool.dma_start(rows[:, :, PAD + N:PAD + NT], zeros).then_inc(pad_written, 16)
            after(pool.memset(magic[:, 0:1], MAGIC))
            after(pool.memset(magic[:, 1:2], -MAGIC))
            after(pool.memset(bsel[:, :], 0.0))
            for b in range(B):
                after(pool.memset(bsel[SEG * b:SEG * b + SEG, b:b + 1], 1.0))
            after(pool.iota(iota1[:, :], pattern=[[1, N]], base=1, channel_multiplier=0,
                            allow_small_or_imprecise_dtypes=True))
            after(pool.memset(padm[:, :], UP))
            for b in range(B):
                q = padm[SEG * b:SEG * b + SEG, :]
                after(pool.affine_select(out=q, in_=q, compare_op=ALU.is_gt, fill=0.0, base=NT - TB - N + 1,
                                         pattern=[[1, TB]], channel_multiplier=-SKEW))
            pool.wait_ge(pad_written, 32)
            after(pool.memset(dring[:, :, W, :], 0.0))
            for b in range(B):
                q = dring[SEG * b:SEG * b + SEG, :, W, :]
                after(pool.affine_select(out=q, in_=q, compare_op=ALU.not_equal, fill=BIG, base=1 - SEG,
                                         pattern=[[0, 2], [0, TB]], channel_multiplier=1))
            pool.wait_ge(xt_in_psum, NTILE)
            pool.wait_ge(bb_ready, NTILE)
            pool.memset(choice[:, :, W:W + 1], 0.0).then_inc(lanes_ready, 1)
            pool.sem_inc(choice_ready, 2)
            for k in range(NBLK - 1):
                rows = slice(TB * (k % 2), TB * (k % 2) + TB)
                pool.wait_ge(fwd_block, k + 2)
                if k >= 2:
                    pool.wait_ge(choice_written[k % 2], 16 * (k // 2))
                after(pool.tensor_scalar(up_better[:, rows, :], up_better[:, rows, :], DIAG, None, ALU.add))
                pool.tensor_tensor(choice[:, rows, 0:W], up_better[:, rows, :], left_worse[:, rows, :],
                                   ALU.mult).then_inc(choice_ready, 1)
            for n in range(3 * KC):
                pool.wait_ge(w_high, n + 1)
                at = (slice(None), n // KC, slice(None), slice(P * (n % KC), P * (n % KC) + P))
                pool.tensor_tensor(wT[1][at], wfull[:, n % 2].rearrange("p (k t) -> p k t", k=KC),
                                   wT[0][at].bitcast(FP32), ALU.subtract).then_inc(w_split, 1)

            def rest_part(u):
                at, src = slots(u), ctx_rows(u)
                for i in range(UC):
                    pool.wait_ge(hi_ready, UC * u + i + 1)
                    pool.tensor_tensor(src[:, i], src[:, i], parts[:, at[i], 0], ALU.subtract)\
                        .then_inc(rest_ready, 1)

            def third_part(u):
                at, src = slots(u), ctx_rows(u)
                for i in range(UC):
                    pool.wait_ge(mid_ready, UC * u + i + 1)
                    pool.tensor_tensor(parts[:, at[i], 2], src[:, i], parts[:, at[i], 1], ALU.subtract)\
                        .then_inc(lo_ready, 1)

            for u in range(AHEAD):
                rest_part(u)
                if u < AHEAD - 1:
                    third_part(u)
            for u in range(EARLY):
                third_part(u + AHEAD - 1)
                for m in range(JT * u, JT * u + JT):
                    tile = m % NTILE
                    pool.wait_ge(early_taken, m + 1)
                    pool.wait_ge(x_loaded[tile // GT], 32)
                    if u >= B:
                        pool.wait_ge(early_added, m - NTILE + 1)
                    pool.tensor_tensor(acc[:, tile], acc[:, tile], etmp[:, m % 4], ALU.add).then_inc(early_added, 1)
                rest_part(u + AHEAD)
            third_part(EARLY + AHEAD - 1)

            def low_mix(g, m, dst):
                for h in range(2):
                    n = 4 * g + 2 * m + h
                    pool.wait_ge(mix_high, n + 1)
                    pool.tensor_tensor(dst[1][:, 2 * h:2 * h + 2], mix[:, 2 * h:2 * h + 2],
                                       dst[0][:, 2 * h:2 * h + 2].bitcast(FP32), ALU.subtract).then_inc(mix_split, 1)

            low_mix(0, 0, xk)
            low_mix(0, 1, xr)
            for g in range(FG):
                for h in range(2):
                    n = 2 * g + h
                    pool.wait_ge(k_high, n + 1)
                    pool.tensor_tensor(kact[1][:, 2 * h:2 * h + 2], krelu[h].rearrange("p (k t) -> p k t", t=FW),
                                       kact[0][:, 2 * h:2 * h + 2].bitcast(FP32), ALU.subtract).then_inc(k_ready, 1)
                if g + 1 < FG:
                    low_mix(g + 1, 0, xk)
                    low_mix(g + 1, 1, xr)
                if BUILD_AFTER.get(g) == B - 1:
                    rest_part(len(UNITS) - 1)
                    third_part(len(UNITS) - 1)

        @block.scalar
        def _(act):
            def square_rows(n):
                rows = D_BLOCKS[n][1]
                act.wait_ge(ctx_loaded, 16 * (n + 1))
                if n:
                    act.wait_ge(aat_in_psum, n)
                for b in range(B):
                    if B * n + b:
                        act.wait_ge(aa_ready, B * n + b)
                    act.activation(sqj[0:rows], ctxn[0:rows, b], ACT.Square, accum_out=aa[0:rows, b:b + 1])\
                        .then_inc(aa_ready, 1)

            def take_rows(n, batches):
                rows = D_BLOCKS[n][1]
                if n >= 2:
                    act.wait_ge(d_in_psum, 2 * B * (n - 1))
                for b in batches:
                    act.wait_ge(ctxt_in_psum, B * n + b + 1)
                    act.activation(ctxT[n % 2][:, :, IB * b:IB * b + rows],
                                   ps[4 + b % 2][:, :].rearrange("p (k t) -> p k t", k=KC)[:, :, 0:rows], ACT.Copy)\
                       .then_inc(ctxt_ready, 1)

            def take_squares(n):
                rows = D_BLOCKS[n][1]
                act.wait_ge(aat_in_psum, n + 1)
                act.activation(aaT[:, n % 2, 0:rows], ps[6][0:B, 0:rows], ACT.Copy, scale=-0.5).then_inc(aat_ready, 1)

            def squared_distances(n, b, h):
                o = B * n + b
                rows = D_BLOCKS[n][1]
                if o:
                    act.wait_ge(d_staged, o)
                act.wait_ge(d_in_psum, 2 * o + h + 1)
                for q in range(4):
                    g = 4 * h + q
                    last = act.activation(drelu[:, g, 0:rows], ps[2 * (b % 2) + h][:, IB * q:IB * q + rows], ACT.Relu,
                                          bias=bb[:, JT * b + g:JT * b + g + 1], scale=-2.0)
                last.then_inc(d_relu_done, 1)

            def distances_out(n, b):
                o = B * n + b
                i, rows = D_BLOCKS[n]
                act.wait_ge(d_relu_done, 2 * (o + 1))
                if o >= 2:
                    act.wait_ge(d_written[o % 2], 16 * (o // 2))
                act.activation(dstage[:, o % 2, :, 0:rows], drelu[:, :, 0:rows], ACT.Sqrt, bias=tiny[:, 0:1])\
                    .then_inc(d_staged, 1)
                act.wait_ge(d_staged, o + 1)
                act.dma_start(d_h[b, :, :, PAD + i:PAD + i + rows], dstage[:, o % 2, :, 0:rows])\
                   .then_inc(d_written[o % 2], 16)

            act.wait_ge(const_ready, 1)
            take_rows(0, range(B))

            def first_deviation(g):
                act.wait_ge(stats_ready, g + 1)
                if g >= 2:
                    act.wait_ge(xn_ready, GT * (g - 1))
                act.activation(sd[:, g % 2], mv[:, g % 2, :, 1], ACT.Sqrt, bias=eps[:, 0:1]).then_inc(sd_ready, 1)

            first_deviation(0)
            square_rows(0)
            act.wait_ge(aa_ready, B)
            for g in range(NG + 3):
                for n in range(GT * (g - 1), GT * g) if 1 <= g <= NG else ():
                    act.wait_ge(xn_ready, n + 1)
                    if n:
                        act.wait_ge(bb_ready, n)
                    act.activation(sqj, xs[:, n], ACT.Square,
                                   accum_out=bb[:, n:n + 1]).then_inc(bb_ready, 1)
                    act.wait_ge(xt_in_psum, n + 1)
                    act.activation(xnT[:, :, P * n:P * n + P], ps[4 + n % 2][:, :].rearrange("p (k t) -> p k t", k=KC),
                                   ACT.Copy).then_inc(xt_ready, 1)
                if g < NG - 1:
                    first_deviation(g + 1)
                if g == 1:
                    take_squares(0)
                if g == NG + 1:
                    act.wait_ge(bb_ready, NTILE)
                    square_rows(1)
                if g >= 3:
                    b, h = divmod(g - 3, 2)
                    act.wait_ge(bb_ready, GT * (g - 2))
                    squared_distances(0, b, h)
                    if h:
                        distances_out(0, b)
            for n in range(1, NIB):
                more = n + 1 < NIB
                for b in range(B):
                    squared_distances(n, b, 0)
                    if more and b == 1:
                        take_rows(n + 1, range(0, 2))
                    squared_distances(n, b, 1)
                    distances_out(n, b)
                    if more and b == 0:
                        square_rows(n + 1)
                    if more and b == 1:
                        take_rows(n + 1, range(2, B))
                        take_squares(n + 1)
            for n in range(3 * KC):
                act.wait_ge(w_in_psum, n + 1)
                if n >= 2:
                    act.wait_ge(w_split, n - 1)
                act.activation(wfull[:, n % 2], ps[4 + n % 2][:, :], ACT.Copy).then_inc(w_taken, 1)
                act.wait_ge(w_taken, n + 1)
                act.activation(wT[0][:, n // KC, :, P * (n % KC):P * (n % KC) + P],
                               wfull[:, n % 2].rearrange("p (k t) -> p k t", k=KC), ACT.Copy).then_inc(w_high, 1)
            act.wait_ge(lanes_ready, 1)

            def first_part(u):
                at, src = slots(u), ctx_rows(u)
                act.wait_ge(ctxb_loaded[u % 2], 16 * (u // 2 + 1))
                if u - UR >= EARLY:
                    act.wait_ge(exp_in_psum, JT * (u - UR - EARLY + 1))
                elif u >= UR:
                    act.wait_ge(early_in_psum, JT * (u - UR + 1))
                for i in range(UC):
                    act.activation(parts[:, at[i], 0], src[:, i], ACT.Copy).then_inc(hi_ready, 1)

            def second_part(u):
                at, src = slots(u), ctx_rows(u)
                for i in range(UC):
                    act.wait_ge(rest_ready, UC * u + i + 1)
                    act.activation(parts[:, at[i], 1], src[:, i], ACT.Copy).then_inc(mid_ready, 1)

            def take_early(u):
                for m in range(JT * u, JT * u + JT):
                    act.wait_ge(early_in_psum, m + 1)
                    if m >= 4:
                        act.wait_ge(early_added, m - 3)
                    act.activation(etmp[:, m % 4], ps[EBANK[m % 4]][:, :], ACT.Copy).then_inc(early_taken, 1)

            steps = [0]

            def after(ins):
                steps[0] += 1
                ins.then_inc(dist_step, 1)
                act.wait_ge(dist_step, steps[0])

            def early_path(u):
                b = u % B
                if b == 0:
                    act.wait_ge(path_in_psum, 1 + u // B)
                    after(act.activation(path[:, :, :, :], ps[4][:, 0:2 * UC * B]
                                         .rearrange("p (q i b) -> p q i b", q=2, i=UC), ACT.Copy))
                if u >= UR:
                    act.wait_ge(early_in_psum, JT * (u - UR + 1))
                for i in range(UC):
                    after(act.activation(dist, iota1[:, :], ACT.Abs, bias=path[:, 0, i, b:b + 1], scale=2.0))
                    after(act.activation(dist, dist, ACT.Relu, bias=path[:, 1, i, b:b + 1]))
                    act.activation(pm[:, slots(u)[i]], dist, ACT.Relu, bias=one[:, 0:1], scale=-1.0)\
                        .then_inc(pm_ready, 1)
                    act.wait_ge(pm_ready, UC * u + i + 1)

            for k in range(NBLK):
                act.wait_ge(cnt_in_psum, 2 * k + 1)
                if k >= 2:
                    act.wait_ge(cnt_written[k % 2], 16 * (k // 2))
                act.activation(cnt[:, k % 2, 0, :], ps[0][:, 0:TB], ACT.Copy).then_inc(cnt_rounded, 1)
                act.wait_ge(cnt_in_psum, 2 * k + 2)
                if k:
                    act.wait_ge(cnt_rounded, 2 * k)
                act.activation(cmid[:, :], ps[1][:, 0:TB], ACT.Identity, bias=magic[:, 0:1], scale=1.0 / DIAG)\
                   .then_inc(cnt_taken, 1)
                act.wait_ge(cnt_taken, k + 1)
                act.activation(cnt[:, k % 2, 1, :], cmid[:, :], ACT.Identity, bias=magic[:, 1:2])\
                   .then_inc(cnt_rounded, 1)
                if k == 1:
                    for u in range(AHEAD):
                        first_part(u)
                        if u < AHEAD - 1:
                            second_part(u)
                for u in UNITS_AT[k]:
                    early_path(u)
                for u in UNITS_AT[k]:
                    second_part(u + AHEAD - 1)
                    take_early(u)
                    first_part(u + AHEAD)
            second_part(EARLY + AHEAD - 1)

            def deviation(g):
                act.wait_ge(stats2_ready, g + 1)
                if g >= 2:
                    act.wait_ge(xn2_ready, FT * (g - 1))
                act.activation(sd[:, g % 2, 0:FT], mv[:, g % 2, 0:FT, 1], ACT.Sqrt, bias=eps[:, 0:1])\
                    .then_inc(sd2_ready, 1)

            def take_transposes(g):
                act.wait_ge(border_ready, g + 1)
                for n in range(FT * g, FT * g + FT):
                    act.wait_ge(t2_in_psum, n + 1)
                    act.activation(xT[:, :, 1 + P * (n % FT):1 + P * (n % FT) + P],
                                   ps[2 + n % 2][:, :].rearrange("p (k t) -> p k t", k=KC), ACT.Copy)\
                       .then_inc(t2_ready, 1)

            def high_mix(g, m, dst):
                if g:
                    act.wait_ge(r_in_psum if m else k_in_psum, FT * g)
                for h in range(2):
                    n = 4 * g + 2 * m + h
                    act.wait_ge(mix_ready, 2 * (n + 1))
                    act.activation(dst[0][:, 2 * h:2 * h + 2], mix[:, 2 * h:2 * h + 2], ACT.Copy).then_inc(mix_high, 1)

            def sigmoid(n):
                act.wait_ge(r_in_psum, n + 1)
                if n >= 2:
                    act.wait_ge(y_ready, n - 1)
                act.activation(sig[n % 2], ps[6][:, :], ACT.Sigmoid).then_inc(sig_ready, 1)

            deviation(0)
            take_transposes(0)
            high_mix(0, 0, xk)
            high_mix(0, 1, xr)
            deviation(1)
            for g in range(FG):
                for h in range(2):
                    n = 2 * g + h
                    act.wait_ge(k_in_psum, n + 1)
                    if g:
                        act.wait_ge(k_ready, n - 1)
                    act.activation(krelu[h], ps[4 + h][:, :], ACT.Relu).then_inc(k_relu_done, 1)
                    act.wait_ge(k_relu_done, n + 1)
                    act.activation(krelu[h], krelu[h], ACT.Square).then_inc(k_squared, 1)
                    act.wait_ge(k_squared, n + 1)
                    if g:
                        act.wait_ge(v_in_psum, FT * g)
                    act.activation(kact[0][:, 2 * h:2 * h + 2], krelu[h].rearrange("p (k t) -> p k t", t=FW), ACT.Copy)\
                       .then_inc(k_high, 1)
                if g + 1 < FG:
                    take_transposes(g + 1)
                    high_mix(g + 1, 0, xk)
                sigmoid(FT * g)
                if g + 2 < FG:
                    deviation(g + 2)
                sigmoid(FT * g + 1)
                if g + 1 < FG:
                    high_mix(g + 1, 1, xr)
                if BUILD_AFTER.get(g) == B - 1:
                    first_part(len(UNITS) - 1)
                    second_part(len(UNITS) - 1)

        @block.tensor
        def _(pe):
            def transpose_rows(n, batches):
                rows = D_BLOCKS[n][1]
                pe.wait_ge(ctx_loaded, 16 * (n + 1))
                for b in batches:
                    if B * n + b >= 2:
                        pe.wait_ge(ctxt_ready, B * n + b - 1)
                    for k in range(KC):
                        last = pe.transpose(ps[4 + b % 2][:, P * k:P * k + rows], ctxn[0:rows, b, P * k:P * k + P],
                                            ident[0:rows, 0:rows])
                    last.then_inc(ctxt_in_psum, 1)

            def transpose_squares(n):
                rows = D_BLOCKS[n][1]
                pe.wait_ge(aa_ready, B * (n + 1))
                if n:
                    pe.wait_ge(aat_ready, n)
                pe.transpose(ps[6][0:B, 0:rows], aa[0:rows, :], ident[0:rows, 0:rows]).then_inc(aat_in_psum, 1)

            def wait_rows(n):
                pe.wait_ge(ctxt_ready, B * (n + 1))
                pe.wait_ge(aat_ready, n + 1)

            def distances(n, b, h, q):
                rows = D_BLOCKS[n][1]
                o = 2 * (B * n + b) + h
                if o >= 4 and q == 0:
                    pe.wait_ge(d_relu_done, o - 3)
                dst = ps[2 * (b % 2) + h][:, IB * q:IB * q + rows]
                j = N * b + P * (GT * h + q)
                for k in range(KC):
                    pe.matmul(dst, xnT[:, k, j:j + P], ctxT[n % 2][:, k, IB * b:IB * b + rows], start=(k == 0), stop=False)
                last = pe.matmul(dst, bsrow[:, b, :], aaT[:, n % 2, 0:rows], start=False, stop=True)
                if q == GT - 1:
                    last.then_inc(d_in_psum, 1)

            pe.wait_ge(const_ready, 1)
            transpose_rows(0, range(B))
            pe.wait_ge(ctxt_ready, B)
            for n in range(NTILE + GT):
                if n < NTILE:
                    pe.wait_ge(xn_ready, n + 1)
                    if n >= 2:
                        pe.wait_ge(xt_ready, n - 1)
                    for k in range(KC):
                        last = pe.transpose(ps[4 + n % 2][:, P * k:P * k + P], xs[:, n, P * k:P * k + P],
                                            ident[:, :])
                    last.then_inc(xt_in_psum, 1)
                if n == GT - 1:
                    transpose_squares(0)
                if n >= GT:
                    wait_rows(0)
                    g, q = divmod(n - GT, GT)
                    pe.wait_ge(xt_ready, n - GT + 1)
                    distances(0, g // 2, g % 2, q)
            transpose_rows(1, range(B))
            transpose_squares(1)
            for n in range(1, NIB):
                wait_rows(n)
                for g in range(2 * B):
                    if g == 3 and n + 1 < NIB:
                        transpose_rows(n + 1, range(0, 2))
                    if g == 4 and n + 1 < NIB:
                        transpose_rows(n + 1, range(2, B))
                        transpose_squares(n + 1)
                    for q in range(GT):
                        distances(n, g // 2, g % 2, q)
            for n in range(3 * KC):
                pe.wait_ge(w_loaded, 16 * (n // KC + 1))
                if n >= 2:
                    pe.wait_ge(w_taken, n - 1)
                for k in range(KC):
                    last = pe.transpose(ps[4 + n % 2][:, P * k:P * k + P], wnat[:, n % KC, P * k:P * k + P],
                                        ident[:, :])
                last.then_inc(w_in_psum, 1)

            def row_counts(stage):
                pe.wait_ge(cun_loaded, 16 * B * (stage + 1))
                if stage:
                    pe.wait_ge(pm_ready, UC * (B * (stage - 1) + 1))
                for q in range(2):
                    for i in range(UC):
                        dst = ps[4][:, (UC * q + i) * B:(UC * q + i + 1) * B]
                        rows = [cun[:, a, P * i:P * i + P] for a in range(2)]
                        if stage == len(STAGES) - 1:
                            last = pe.matmul(dst, rows[q], bsel[:, :], start=True, stop=True)
                        else:
                            pe.matmul(dst, rows[0], nbsel[:, :], start=True, stop=False)
                            last = pe.matmul(dst, rows[1], bsel[:, :] if q else nbsel[:, :], start=False, stop=True)
                last.then_inc(path_in_psum, 1)

            def early_expand(u):
                pe.wait_ge(pm_ready, UC * (u + 1))
                pe.wait_ge(lo_ready, UC * (u + 1))
                at = slots(u)
                for m in range(JT * u, JT * u + JT):
                    if m >= 4:
                        pe.wait_ge(early_taken, m - 3)
                    j = P * (m % JT)
                    for q in range(3):
                        for i in at:
                            last = pe.matmul(ps[EBANK[m % 4]][:, :], pm[:, i, j:j + P], parts[:, i, q],
                                             start=(q == 0 and i == at[0]), stop=(q == 2 and i == at[-1]))
                    last.then_inc(early_in_psum, 1)

            pe.wait_ge(d_relu_done, 2 * B * NIB)
            pe.wait_ge(w_taken, 3 * KC)
            pe.wait_ge(lanes_ready, 1)
            pe.sem_inc(ring_free, 1)
            for k in range(NBLK):
                pe.wait_ge(bwd_block, k + 1)
                if k:
                    pe.wait_ge(cnt_rounded, 2 * k)
                at = TB * (k % 2)
                for q, (ring, first) in enumerate(((tring, 0), (ering, 1))):
                    for j in range(W):
                        rows = ring[:, at + TB - 1:at - 1 if at else None:-1, first + j]
                        last = pe.matmul(ps[q][:, 0:TB], identb[:, :], rows, start=(j == 0), stop=(j == W - 1))
                    last.then_inc(cnt_in_psum, 1)
                pe.wait_ge(cnt_in_psum, 2 * (k + 1))
                pe.sem_inc(ring_free, 1)
                if k in STAGE_BLOCK:
                    row_counts(STAGE_BLOCK.index(k))
                for u in UNITS_AT[k]:
                    early_expand(u)

            def expand(g):
                b = g // GB
                u = EARLY + b
                pe.wait_ge(lo_ready, UC * (u + 1))
                at = slots(u)
                for n in range(FT * g, FT * g + FT):
                    if n >= 2:
                        pe.wait_ge(xmid_ready, n - 1)
                    j = P * (n % JT)
                    for i in at:
                        pe.wait_ge(late_pm_ready, UC * b + i - at[0] + 1)
                        for q in range(3):
                            last = pe.matmul(ps[n % 2][:, :], pm[:, i, j:j + P], parts[:, i, q],
                                             start=(q == 0 and i == at[0]), stop=(q == 2 and i == at[-1]))
                    last.then_inc(exp_in_psum, 1)

            def transposes(g):
                for n in range(FT * g, FT * g + FT):
                    pe.wait_ge(xn2_ready, n + 1)
                    if n >= 2:
                        pe.wait_ge(t2_ready, n - 1)
                    for k in range(KC):
                        last = pe.transpose(ps[2 + n % 2][:, P * k:P * k + P], xn2[:, n % FT, P * k:P * k + P],
                                            ident[:, :])
                    last.then_inc(t2_in_psum, 1)

            def product(dst, a, at_a, b, at_b):
                terms = [(i, j, c) for c in range(KC) for i, j in ((0, 0), (0, 1), (1, 0))]
                for i, j, c in terms:
                    last = pe.matmul(dst, a[i][at_a(c)], b[j][at_b(c)], start=((i, j, c) == terms[0]),
                                     stop=((i, j, c) == terms[-1]))
                return last

            every = slice(None)
            pe.wait_ge(cnt_rounded, 2 * NBLK)
            pe.wait_ge(early_taken, JT * EARLY)
            pe.wait_ge(path_ready, 1)
            expand(0)
            expand(1)
            transposes(0)
            for g in range(FG):
                pe.wait_ge(mix_split, 4 * g + 2)
                for h in range(2):
                    if g:
                        pe.wait_ge(k_relu_done, 2 * (g - 1) + h + 1)
                    for q in range(2):
                        m = P * (2 * h + q)
                        last = product(ps[4 + h][:, FW * q:FW * q + FW], wT, lambda c: (every, 1, c, slice(m, m + P)),
                                       xk, lambda c: (every, c))
                    last.then_inc(k_in_psum, 1)
                if g + 1 < FG:
                    transposes(g + 1)
                if g + 2 < FG:
                    expand(g + 2)
                pe.wait_ge(mix_split, 4 * g + 4)
                for n in range(FT * g, FT * g + FT):
                    t = P * (n % FT)
                    if n:
                        pe.wait_ge(sig_ready, n)
                    product(ps[6][:, :], xr, lambda c: (every, c, slice(t, t + P)),
                            wT, lambda c: (every, 0, c)).then_inc(r_in_psum, 1)
                    pe.wait_ge(k_ready, 2 * (g + 1))
                    if n:
                        pe.wait_ge(rv_ready, n)
                    product(ps[7][:, :], kact, lambda c: (every, c, slice(t, t + P)),
                            wT, lambda c: (every, 2, c)).then_inc(v_in_psum, 1)

        @block.vector
        def _(dve):
            steps = [0]

            def after(ins):
                steps[0] += 1
                ins.then_inc(dve_step, 1)
                dve.wait_ge(dve_step, steps[0])

            def stats(src, g, tiles, ready):
                for q in range(tiles):
                    last = dve.bn_stats(stat[:, q], src[:, q])
                after(last)
                for q in range(tiles):
                    last = dve.bn_aggr(mv[:, g % 2, q], stat[:, q])
                after(last)
                dve.sem_inc(ready, 1)

            def normalise(dst, src, g, tiles, sd_sem, ready):
                dve.wait_ge(sd_sem, g + 1)
                after(dve.reciprocal(rstd[:, g % 2, 0:tiles], sd[:, g % 2, 0:tiles]))
                for q in range(tiles):
                    dve.tensor_scalar(dst[:, q], src[:, q], mv[:, g % 2, q, 0:1], rstd[:, g % 2, q:q + 1],
                                      ALU.subtract, ALU.mult).then_inc(ready, 1)

            dve.wait_ge(const_ready, 1)
            dve.wait_ge(mu_loaded, 32)
            after(dve.tensor_scalar(omu[:, :, :], mu[:, :, :], -1.0, 1.0, ALU.mult, ALU.add))
            for g in range(NG + 1):
                if g < NG:
                    dve.wait_ge(x_loaded[g], 16)
                    stats(xs[:, GT * g:GT * g + GT], g, GT, stats_ready)
                if g:
                    tiles = xs[:, GT * (g - 1):GT * g]
                    normalise(tiles, tiles, g - 1, GT, sd_ready, xn_ready)

            rows = D_BLOCKS[1][1]
            for b in range(B):
                dve.wait_ge(ctxt_in_psum, B + b + 1)
                dve.tensor_copy(ctxT[1][:, :, IB * b:IB * b + rows],
                                ps[4 + b % 2][:, :].rearrange("p (k t) -> p k t", k=KC)[:, :, 0:rows])\
                   .then_inc(ctxt_ready, 1)
            dve.wait_ge(aat_in_psum, 2)
            dve.tensor_scalar(aaT[:, 1, 0:rows], ps[6][0:B, 0:rows], -0.5, None, ALU.mult).then_inc(aat_ready, 1)

            after(dve.memset(rrow[:, :, :], BIG))
            after(dve.memset(mrow[:, :, :], BIG))
            for b in range(B):
                after(dve.memset(rrow[SEG * b:SEG * b + 1, RR - 1, 0:1], 0.0))
            dve.wait_ge(lanes_ready, 1)
            dve.sem_clear(dve_step)
            with dve.Fori(0, NT // STEPS) as it:
                for t in range(STEPS):
                    r = t % RR
                    if t % TB == 0:
                        dve.wait_ge(d_loaded[t // TB], it * (16 * B) + 16 * B)
                    if t:
                        dve.wait_ge(dve_step, 4 * t - 1)
                    if t % TB == 2:
                        dve.wait_ge(choice_ready, it * 2 + t // TB + 1)
                    if t % TB == 3:
                        dve.sem_inc(fwd_block, 1)
                    dve.tensor_tensor(mrow[:, r, 0:W], rrow[:, (r - 1) % RR, 1:W + 1], rrow[:, (r - 1) % RR, 0:W],
                                      ALU.min).then_inc(dve_step, 1)
                    dve.stream_shuffle(rrow[:, (r + 1) % RR, 0:1], rrow[:, (r - 1) % RR, W + 1:W + 2],
                                       [SEG - 1] + list(range(SEG - 1))).then_inc(dve_step, 1)
                    dve.wait_ge(dve_step, 4 * t + 1)
                    dve.tensor_tensor_scan(rrow[:, r, 1:W + 2], mrow[:, r, :], dring[:, t // TB, :, t % TB],
                                           rrow[:, r, 0:1], ALU.min, ALU.add).then_inc(dve_step, 1)
                    if t % 2 == 0:
                        dve.tensor_tensor(pair_down(up_better, t - 2), pair(rrow, r - 3, 1, W + 1),
                                          pair(rrow, r - 3, 0, W), ALU.is_lt).then_inc(dve_step, 1)
                    else:
                        dve.tensor_tensor(pair_down(left_worse, t - 3), pair(mrow, r - 3, 0, W),
                                          pair(rrow, r - 3, 0, W), ALU.is_le).then_inc(dve_step, 1)
                dve.wait_ge(dve_step, 4 * STEPS)
                dve.sem_clear(dve_step)
            dve.wait_ge(choice_written[1], 16 * (NBLK // 2 - 1))
            dve.scalar_tensor_tensor(choice[:, TB:STEPS, 0:W], up_better[:, TB:STEPS, :], DIAG,
                                     left_worse[:, TB:STEPS, :], ALU.add, ALU.mult).then_inc(dve_step, 1)
            for a in range(2):
                dve.wait_ge(d_written[a], 16 * B * NIB // 2)
            dve.memset(tring[:, 0:1, 0:W], 1.0).then_inc(dve_step, 1)
            dve.memset(tring[:, :, W:W + 1], 1.0).then_inc(dve_step, 1)
            dve.memset(ering[:, 0:SKEW, :], 0.0).then_inc(dve_step, 1)
            dve.memset(ering[:, STEPS - 1:STEPS, :], 0.0).then_inc(dve_step, 1)
            dve.wait_ge(dve_step, 5)
            dve.tensor_tensor(choice[:, TB:STEPS, 0:W], choice[:, TB:STEPS, 0:W],
                              padm[:, :].unsqueeze(2).broadcast_to([P, TB, W]), ALU.max).then_inc(dve_step, 1)
            for b in range(B):
                dve.memset(tring[SEG * b:SEG * b + 1, :, W:W + 1], 0.0).then_inc(dve_step, 1)
            dve.wait_ge(dve_step, 6 + B)
            dve.wait_ge(choice_ready, NBLK + 1)
            for a in range(2):
                dve.sem_inc(choice_loaded[a], 16)
            dve.sem_inc(fwd_done, 1)
            dve.sem_clear(dve_step)

            with dve.Fori(0, NT // STEPS) as it:
                for u in range(STEPS):
                    if u:
                        dve.wait_ge(dve_step, 3 * u)
                    if u % TB == 0:
                        dve.wait_ge(choice_loaded[(u // TB + 1) % 2], it * 16 + 16)
                        if u:
                            dve.sem_inc(bwd_block, 1)
                    if u % TB == TB - 3:
                        dve.wait_ge(ring_free, it * 2 + (u // TB + 1))
                    dve.tensor_tensor_scan(ering[:, u, 1:W + 2], choice[:, STEPS - 1 - u, :], tring[:, u, :],
                                           ering[:, u, 0:1], ALU.max, ALU.mult).then_inc(dve_step, 1)
                    dve.stream_shuffle(ering[:, (u + 1) % STEPS, 0:1], ering[:, (u - 1) % STEPS, W + 1:W + 2],
                                       list(range(1, SEG)) + [0]).then_inc(dve_step, 1)
                    dve.wait_ge(dve_step, 3 * u + 1)
                    dve.scalar_tensor_tensor(tring[:, (u + 1) % STEPS, 0:W], ering[:, u, 1:W + 1], DIAG,
                                             ering[:, u, 0:W], ALU.is_gt, ALU.logical_or).then_inc(dve_step, 1)
                dve.wait_ge(dve_step, 3 * STEPS)
                dve.sem_inc(bwd_block, 1)
                dve.sem_clear(dve_step)
            steps[0] = 0
            dve.wait_ge(path_in_psum, len(STAGES))
            dve.wait_ge(pm_ready, UC * EARLY)
            after(dve.tensor_copy(path[:, :, :, :],
                                  ps[4][:, 0:2 * UC * B].rearrange("p (q i b) -> p q i b", q=2, i=UC)))
            dve.sem_inc(path_ready, 1)

            def build(b):
                if b < UR:
                    dve.wait_ge(early_in_psum, JT * (EARLY + b - UR + 1))
                else:
                    dve.wait_ge(exp_in_psum, JT * (b - UR + 1))
                for i in range(UC):
                    n = UC * b + i
                    if n >= 2:
                        dve.wait_ge(late_pm_ready, n - 1)
                    after(dve.tensor_scalar(tpre[:, n % 2], iota1[:, :], path[:, 1, i, b:b + 1], None, ALU.is_ge))
                    dve.scalar_tensor_tensor(pm[:, slots(EARLY + b)[i]], iota1[:, :], path[:, 0, i, b:b + 1],
                                             tpre[:, n % 2], ALU.is_le, ALU.mult).then_inc(late_pm_ready, 1)

            def mid(g):
                if g == 0:
                    dve.wait_ge(early_added, JT * EARLY)
                for n in range(FT * g, FT * g + FT):
                    dve.wait_ge(exp_in_psum, n + 1)
                    dve.tensor_tensor(acc[:, n], acc[:, n], ps[n % 2][:, :], ALU.add)\
                       .then_inc(xmid_ready, 1)
                dve.wait_ge(xmid_ready, FT * (g + 1))
                stats(acc[:, FT * g:FT * g + FT], g, FT, stats2_ready)

            def mid_norm(g):
                if g:
                    dve.wait_ge(t2_in_psum, FT * g)
                normalise(xn2, acc[:, FT * g:FT * g + FT], g, FT, sd2_ready, xn2_ready)

            def border(g):
                if g % GB == 0:
                    after(dve.memset(xT[:, :, 0:1], 0.0))
                else:
                    after(dve.tensor_copy(xT[:, :, 0:1], xT[:, :, FW:FW + 1]))
                dve.sem_inc(border_ready, 1)

            def token_shift(g, k):
                m = 1 - k
                dve.wait_ge(t2_ready, FT * (g + 1))
                if 2 * g + k:
                    dve.wait_ge(mix_split, 4 * g + 2 * k)
                for c in range(KC):
                    dve.tensor_scalar(mix[:, c], xT[:, c, 0:FW], omu[:, m, c:c + 1], None, ALU.mult)\
                       .then_inc(mix_half, 1)
                for c in range(KC):
                    dve.wait_ge(mix_half, KC * (2 * g + k) + c + 1)
                    dve.scalar_tensor_tensor(mix[:, c], xT[:, c, 1:FW + 1], mu[:, m, c:c + 1], mix[:, c],
                                             ALU.mult, ALU.add).then_inc(mix_ready, 1)
                dve.wait_ge(mix_ready, KC * (2 * g + k + 1))

            def output(n):
                dve.wait_ge(sig_ready, n + 1)
                dve.wait_ge(v_in_psum, n + 1)
                dve.tensor_tensor(sig[n % 2], ps[7][:, :], sig[n % 2], ALU.mult).then_inc(rv_ready, 1)
                dve.wait_ge(rv_ready, n + 1)
                dve.tensor_tensor(acc[:, n], acc[:, n], sig[n % 2], ALU.add).then_inc(y_ready, 1)

            build(0)
            mid(0)
            mid_norm(0)
            border(0)
            token_shift(0, 0)
            token_shift(0, 1)
            border(1)
            mid(1)
            mid_norm(1)
            for g in range(FG):
                if g + 1 < FG:
                    token_shift(g + 1, 0)
                if g + 2 < FG:
                    mid(g + 2)
                output(FT * g)
                if g + 2 < FG:
                    mid_norm(g + 2)
                if g + 1 < FG:
                    token_shift(g + 1, 1)
                if g + 2 < FG:
                    border(g + 2)
                output(FT * g + 1)
                if g in BUILD_AFTER:
                    build(BUILD_AFTER[g])


_INS = ["x", "ctx_1024", "L0_ffn_W_r", "L0_ffn_W_k", "L0_ffn_W_v", "L0_ffn_mu_r", "L0_ffn_mu_k"]


def kernel(**inputs):
    import numpy as _np
    import concourse.bacc as _bacc
    from concourse import mybir as _mybir
    from concourse.bass_utils import run_bass_kernel_spmd as _run

    nc = _bacc.Bacc("TRN2", target_bir_lowering=False, num_devices=1)
    arrays, args = {}, []
    for name in _INS:
        a = _np.ascontiguousarray(inputs[name])
        arrays[f"in_{name}"] = a
        args.append(nc.dram_tensor(f"in_{name}", a.shape, _mybir.dt.from_np(a.dtype), kind="ExternalInput").ap())
    out = nc.dram_tensor("out_y", (4, 1024, 512), _mybir.dt.float32, kind="ExternalOutput").ap()
    dtw_ffn_kernel(nc, *args, out)
    return _run(nc, [arrays], core_ids=[0]).results[0]["out_y"]
```
